# Optimizing a Trainium2 kernel written in Bass

```python
import numpy as np
import jax
import jax.numpy as jnp

def _softmax(x, axis=-1):
    return jax.nn.softmax(x, axis=axis)

def _gelu(x):
    return jax.nn.gelu(x, approximate=True)

def _silu(x):
    return jax.nn.silu(x)

def _sigmoid(x):
    return jax.nn.sigmoid(x)

def _layernorm(x, axis=-1, eps=1e-05):
    m = jnp.mean(x, axis=axis, keepdims=True)
    v = jnp.var(x, axis=axis, keepdims=True)
    return (x - m) / jnp.sqrt(v + eps)

def _scatter_add(tgt, idx, src, axis=0):
    return tgt.at[idx].add(src)

def _segment_sum(src, seg, n):
    return jax.ops.segment_sum(src, seg, n)
kernel_name = 'mk_gps_d1_gnn_r16_ed1417'

def setup_inputs(seed: int=0):
    np.random.seed(seed)
    _w = jnp.asarray

    def _rec_inputs():
        import jax
        import jax.numpy as jnp
        _gk = jax.random.key(seed)
        x = -0.0003713 + 1 * jax.random.normal(jax.random.fold_in(_gk, 1), (3125, 256), jnp.float32)
        _s = jax.random.randint(jax.random.fold_in(_gk, 2), (25000,), 0, 3125, jnp.int32)
        _d = jax.random.randint(jax.random.fold_in(_gk, 3), (25000,), 0, 3125, jnp.int32)
        _loop = jnp.arange(3125, dtype=jnp.int32)
        src = jnp.concatenate([_s, _d, _loop])
        dst = jnp.concatenate([_d, _s, _loop])
        _o = jnp.argsort(dst, stable=True)
        src = src[_o]
        dst = dst[_o]
        edge_weight = jax.random.uniform(jax.random.fold_in(_gk, 12), (53125,), jnp.float32, 0.0, 0.999999)
        return (x, src, dst, edge_weight)
    x, src, dst, edge_weight = _rec_inputs()

    def _L0_gnn_setup():
        import jax, jax.numpy as jnp
        import numpy as np
        N = 3125
        E = 50000
        D = 256
        HD = 128
        LAYERS = 2
        HEADS = 4

        def _spmm(row, col, val, x):
            return jax.ops.segment_sum(val[:, None] * x[col], row, num_segments=N)
        key = jax.random.key(seed)
        ks = jax.random.split(key, 6)
        inputs_emb = jax.random.normal(ks[0], (N, D), dtype=jnp.float32)
        edge_row = jax.random.randint(ks[1], (E,), 0, N, dtype=jnp.int32)
        edge_col = jax.random.randint(ks[2], (E,), 0, N, dtype=jnp.int32)
        edge_val = jax.random.uniform(ks[3], (E,), dtype=jnp.float32)
        W0 = jax.random.normal(ks[4], (HD, D), dtype=jnp.float32) * (1.0 / np.sqrt(D))
        b0 = jnp.zeros((HD,), dtype=jnp.float32)
        W1 = jax.random.normal(ks[5], (HD, HD), dtype=jnp.float32) * (1.0 / np.sqrt(HD))
        b1 = jnp.zeros((HD,), dtype=jnp.float32)
        return {'inputs_emb': inputs_emb, 'W0': W0, 'b0': b0, 'W1': W1, 'b1': b1, 'edge_val': edge_val, 'edge_row': edge_row, 'edge_col': edge_col}
    _L0_gnn_all = _L0_gnn_setup()
    _L0_gnn_in = {k: v for k, v in _L0_gnn_all.items() if k in ('W0', 'b0', 'W1', 'b1')}
    del _L0_gnn_all

    def _L0_mix_setup():
        import jax, jax.numpy as jnp
        import numpy as np
        import math
        EMBED = 256
        HEADS = 4
        HEAD_DIM = EMBED // HEADS
        OUT_DIM = 256
        LN_EPS = 1e-05

        def _qkv_init(key):
            spread = math.sqrt(3.0 / EMBED)
            gain, delta = (0.01, 0.01)
            w = jax.random.uniform(key, (EMBED, EMBED), minval=-spread, maxval=spread) * gain
            return w + delta * jnp.eye(EMBED, dtype=w.dtype)

        def _layer_norm(x, g, b):
            mu = jnp.mean(x, axis=-1, keepdims=True)
            var = jnp.mean(jnp.square(x - mu), axis=-1, keepdims=True)
            return (x - mu) * jax.lax.rsqrt(var + LN_EPS) * g + b

        def _split_heads(x, B, S):
            return x.reshape(B, S, HEADS, HEAD_DIM).transpose(0, 2, 1, 3)
        key = jax.random.key(seed)
        ks = jax.random.split(key, 6)
        seq = jax.random.normal(ks[0], (4, 512, EMBED), dtype=jnp.float32)
        wq = _qkv_init(ks[1])
        wk = _qkv_init(ks[2])
        wv = _qkv_init(ks[3])
        bound = 1.0 / math.sqrt(EMBED)
        wo = jax.random.uniform(ks[4], (OUT_DIM, EMBED), minval=-bound, maxval=bound)
        bo = jax.random.uniform(ks[5], (OUT_DIM,), minval=-bound, maxval=bound)
        ln_k_g = jnp.ones((HEAD_DIM,), jnp.float32)
        ln_k_b = jnp.zeros((HEAD_DIM,), jnp.float32)
        ln_v_g = jnp.ones((HEAD_DIM,), jnp.float32)
        ln_v_b = jnp.zeros((HEAD_DIM,), jnp.float32)
        return {'seq': seq, 'wq': wq, 'wk': wk, 'wv': wv, 'wo': wo, 'bo': bo, 'ln_k_g': ln_k_g, 'ln_k_b': ln_k_b, 'ln_v_g': ln_v_g, 'ln_v_b': ln_v_b}
    _L0_mix_all = _L0_mix_setup()
    _L0_mix_in = {k: v for k, v in _L0_mix_all.items() if k in ('wq', 'wk', 'wv', 'wo', 'bo', 'ln_k_g', 'ln_k_b', 'ln_v_g', 'ln_v_b')}
    del _L0_mix_all

    def _L0_ffn_setup():
        import math
        import jax, jax.numpy as jnp
        import numpy as np
        CAPACITY_FACTOR = 1.25
        key = jax.random.key(seed)
        ks = jax.random.split(key, 5)
        B, L, D, F, E = (8, 512, 256, 1024, 8)
        h = jax.random.normal(ks[0], (B, L, D), dtype=jnp.float32)
        gate_w = jax.random.normal(ks[1], (D, E), dtype=jnp.float32) * 0.02
        gate_b = jnp.zeros((E,), dtype=jnp.float32)
        w1 = jax.random.normal(ks[2], (E, D, F), dtype=jnp.float32) * (1.0 / math.sqrt(D))
        b1 = jnp.zeros((E, F), dtype=jnp.float32)
        w2 = jax.random.normal(ks[3], (E, F, D), dtype=jnp.float32) * (1.0 / math.sqrt(F))
        b2 = jnp.zeros((E, D), dtype=jnp.float32)
        return {'h': h, 'gate_w': gate_w, 'gate_b': gate_b, 'w1': w1, 'b1': b1, 'w2': w2, 'b2': b2}
    _L0_ffn_all = _L0_ffn_setup()
    _L0_ffn_in = {k: v for k, v in _L0_ffn_all.items() if k in ('gate_w', 'gate_b', 'w1', 'b1', 'w2', 'b2')}
    del _L0_ffn_all
    return {'x': x, 'src': src, 'dst': dst, 'edge_weight': edge_weight, 'L0_gnn_W0': _L0_gnn_in['W0'], 'L0_gnn_b0': _L0_gnn_in['b0'], 'L0_gnn_W1': _L0_gnn_in['W1'], 'L0_gnn_b1': _L0_gnn_in['b1'], 'L0_mix_wq': _L0_mix_in['wq'], 'L0_mix_wk': _L0_mix_in['wk'], 'L0_mix_wv': _L0_mix_in['wv'], 'L0_mix_wo': _L0_mix_in['wo'], 'L0_mix_bo': _L0_mix_in['bo'], 'L0_mix_ln_k_g': _L0_mix_in['ln_k_g'], 'L0_mix_ln_k_b': _L0_mix_in['ln_k_b'], 'L0_mix_ln_v_g': _L0_mix_in['ln_v_g'], 'L0_mix_ln_v_b': _L0_mix_in['ln_v_b'], 'L0_ffn_gate_w': _L0_ffn_in['gate_w'], 'L0_ffn_gate_b': _L0_ffn_in['gate_b'], 'L0_ffn_w1': _L0_ffn_in['w1'], 'L0_ffn_b1': _L0_ffn_in['b1'], 'L0_ffn_w2': _L0_ffn_in['w2'], 'L0_ffn_b2': _L0_ffn_in['b2']}

def reference(x, src, dst, edge_weight, L0_gnn_W0, L0_gnn_b0, L0_gnn_W1, L0_gnn_b1, L0_mix_wq, L0_mix_wk, L0_mix_wv, L0_mix_wo, L0_mix_bo, L0_mix_ln_k_g, L0_mix_ln_k_b, L0_mix_ln_v_g, L0_mix_ln_v_b, L0_ffn_gate_w, L0_ffn_gate_b, L0_ffn_w1, L0_ffn_b1, L0_ffn_w2, L0_ffn_b2):
    import jax
    import jax.numpy as jnp

    def _L0_gnn_ref(inputs_emb, W0, b0, W1, b1, edge_val, edge_row, edge_col):
        import jax, jax.numpy as jnp
        import numpy as np
        N = 3125
        E = 50000
        D = 256
        HD = 128
        LAYERS = 2
        HEADS = 4

        def _spmm(row, col, val, x):
            return jax.ops.segment_sum(val[:, None] * x[col], row, num_segments=N)
        weights = [(W0, b0), (W1, b1)]
        h = _spmm(edge_row, edge_col, edge_val, inputs_emb)
        head_outs = []
        for _ in range(HEADS):
            outputs = h
            layer_outs = []
            for l, (W, b) in enumerate(weights):
                z = _spmm(edge_row, edge_col, edge_val, outputs)
                AxW = jax.nn.softmax(z @ W.T + b, axis=1)
                outputs = AxW if l == 0 else jnp.concatenate([AxW, AxW], axis=1)
                layer_outs.append(AxW)
            head_outs.append(jnp.concatenate(layer_outs, axis=1) + h)
        final = jnp.mean(jnp.stack(head_outs), axis=0)
        return jnp.tanh(final)

    def _L0_mix_ref(seq, wq, wk, wv, wo, bo, ln_k_g, ln_k_b, ln_v_g, ln_v_b):
        import jax, jax.numpy as jnp
        import numpy as np
        import math
        EMBED = 256
        HEADS = 4
        HEAD_DIM = EMBED // HEADS
        OUT_DIM = 256
        LN_EPS = 1e-05

        def _qkv_init(key):
            spread = math.sqrt(3.0 / EMBED)
            gain, delta = (0.01, 0.01)
            w = jax.random.uniform(key, (EMBED, EMBED), minval=-spread, maxval=spread) * gain
            return w + delta * jnp.eye(EMBED, dtype=w.dtype)

        def _layer_norm(x, g, b):
            mu = jnp.mean(x, axis=-1, keepdims=True)
            var = jnp.mean(jnp.square(x - mu), axis=-1, keepdims=True)
            return (x - mu) * jax.lax.rsqrt(var + LN_EPS) * g + b

        def _split_heads(x, B, S):
            return x.reshape(B, S, HEADS, HEAD_DIM).transpose(0, 2, 1, 3)
        B, S, _ = seq.shape
        q = _split_heads(seq @ wq.T, B, S)
        k = _split_heads(seq @ wk.T, B, S)
        v = _split_heads(seq @ wv.T, B, S)
        k = _layer_norm(k, ln_k_g, ln_k_b)
        v = _layer_norm(v, ln_v_g, ln_v_b)
        kv = jnp.einsum('bhsd,bhse->bhde', k, v) / S
        ga = jnp.einsum('bhsd,bhde->bhse', q, kv)
        ga = ga.transpose(0, 2, 1, 3).reshape(B, S, EMBED)
        return ga @ wo.T + bo

    def _L0_ffn_ref(h, gate_w, gate_b, w1, b1, w2, b2):
        import math
        import jax, jax.numpy as jnp
        import numpy as np
        CAPACITY_FACTOR = 1.25
        B, L, D = h.shape
        E = gate_w.shape[1]
        T = B * L
        C = max(1, math.ceil(CAPACITY_FACTOR * T / E))
        x = h.reshape(T, D)
        logits = x @ gate_w + gate_b
        probs = jax.nn.softmax(logits, axis=-1)
        idx = jnp.argmax(probs, axis=-1)
        prb = jnp.take_along_axis(probs, idx[:, None], axis=1)[:, 0]
        one_hot = jax.nn.one_hot(idx, E, dtype=jnp.float32)
        pos = (jnp.cumsum(one_hot, axis=0) * one_hot).sum(-1).astype(jnp.int32) - 1
        kept = pos < C
        pos_safe = jnp.where(kept, pos, C)
        buf = jnp.zeros((E, C, D), dtype=h.dtype).at[idx, pos_safe].set(x, mode='drop')
        hmid = jax.nn.relu(jnp.einsum('ecd,edf->ecf', buf, w1) + b1[:, None, :])
        ybuf = jnp.einsum('ecf,efd->ecd', hmid, w2) + b2[:, None, :]
        pos_g = jnp.minimum(pos, C - 1)
        y_tok = ybuf[idx, pos_g] * (prb * kept)[:, None]
        y = y_tok.reshape(B, L, D)
        y = jnp.nan_to_num(y, nan=0.0, posinf=10000.0, neginf=-10000.0)
        return y
    xn = _layernorm(x, axis=-1)
    x = x + _L0_gnn_ref(xn, L0_gnn_W0, L0_gnn_b0, L0_gnn_W1, L0_gnn_b1, edge_weight, src, dst) + _L0_mix_ref(xn[None], L0_mix_wq, L0_mix_wk, L0_mix_wv, L0_mix_wo, L0_mix_bo, L0_mix_ln_k_g, L0_mix_ln_k_b, L0_mix_ln_v_g, L0_mix_ln_v_b)[0]
    x = x + _L0_ffn_ref(_layernorm(x, axis=-1)[None], L0_ffn_gate_w, L0_ffn_gate_b, L0_ffn_w1, L0_ffn_b1, L0_ffn_w2, L0_ffn_b2)[0]
    return x

_drawn_inputs = setup_inputs


def setup_inputs(seed=0):
    import zlib

    import numpy as np

    out = dict(_drawn_inputs(seed))
    spreads = {'L0_gnn_b0': (0.0, 2.0),
     'L0_gnn_b1': (0.0, 2.0),
     'L0_mix_ln_k_g': (1.0, 0.6),
     'L0_mix_ln_k_b': (0.0, 0.8),
     'L0_mix_ln_v_g': (1.0, 0.6),
     'L0_mix_ln_v_b': (0.0, 0.8),
     'L0_ffn_gate_b': (0.0, 0.1),
     'L0_ffn_b1': (0.0, 0.8),
     'L0_ffn_b2': (0.0, 0.606)}
    factors = {'L0_gnn_W0': 15.929,
     'L0_gnn_W1': 64.0,
     'L0_mix_wq': 8.0,
     'L0_mix_wk': 8.0,
     'L0_mix_wv': 7.797,
     'L0_mix_wo': 7.79,
     'L0_mix_bo': 3.949}
    for name, (base, spread) in spreads.items():
        noise = np.random.default_rng([zlib.crc32(name.encode()), seed]).standard_normal(out[name].shape)
        drawn = base * np.exp(spread * noise) if base else spread * noise
        out[name] = jnp.asarray(drawn.astype(out[name].dtype))
    for name, factor in factors.items():
        out[name] = (out[name] * factor).astype(out[name].dtype)
    return out
```

```python
from contextlib import ExitStack, contextmanager

import concourse.bass as bass
from concourse import mybir
from concourse.alu_op_type import AluOpType as ALU

F32 = mybir.dt.float32
BF16 = mybir.dt.bfloat16
F16 = mybir.dt.float16
I32 = mybir.dt.int32
ACT = mybir.ActivationFunctionType
AX_X = mybir.AxisListType.X
ds = bass.ds

N = 3125
E = 53125
D = 256
H = 128
P = 128
NT = 25
NE = 8
CAPX = 489
XS = 512
F = 1024
NH = 8
HD = 64
FMAX = 3.4028234663852886e38
LAST = N - (NT - 1) * P
NP = NT * P
NR = 25
NG = NT * NR
CAP = P
EP = 125
ET = E // EP
B5 = 5
NB = ET // B5
OHW = NG
MAGIC = float(1.5 * 2 ** 23)
CHUNK = 391
EPS = 1e-5
NWL = 18
NTR = 24
PARTS = ((0, 8, 0, 2), (8, 16, 2, 4), (16, NR, 4, 7))
DW = 3
SLOTS = 5


def ge(eng, semaphore, value):
    if not isinstance(value, int) or value > 0:
        eng.wait_ge(semaphore, value)


def tiles(eng, step):
    for j in range(SLOTS):
        step(j, j)
    with eng.Fori(1, NT // SLOTS) as i:
        for s in range(SLOTS):
            step(i * SLOTS + s, s)


def tiles_ahead(eng, ahead, step):
    ahead(0, 0)
    for j in range(SLOTS):
        ahead(j + 1, (j + 1) % SLOTS)
        step(j, j)
    with eng.Fori(1, NT // SLOTS - 1) as i:
        for s in range(SLOTS):
            ahead(i * SLOTS + s + 1, (s + 1) % SLOTS)
            step(i * SLOTS + s, s)
    for s in range(SLOTS):
        j = NT - SLOTS + s
        if j + 1 < NT:
            ahead(j + 1, (s + 1) % SLOTS)
        step(j, s)


def straight_ahead(ahead, step):
    ahead(0, 0)
    for j in range(NT):
        if j + 1 < NT:
            ahead(j + 1, (j + 1) % SLOTS)
        step(j, j % SLOTS)


def graph_program(nc, a, out):
    ctx = ExitStack()
    with ctx:
        def sb(name, shape, dt=F32):
            return ctx.enter_context(nc.sbuf_tensor(name, shape, dt))

        def sem(name):
            return ctx.enter_context(nc.semaphore(name))

        def dram(name, shape, dt=F32):
            return nc.dram_tensor(name, shape, dt, kind="Internal").ap()

        rec_dram = dram("rec_dram", [CAP * NG, 4])
        adj_dram = dram("adj_dram", [NT, P, NP])

        xbuf_dram = dram("xbuf_dram", [NE * XS, D])
        ybuf_dram = dram("ybuf_dram", [NE * XS, D])

        X1 = sb("X1", [P, NT, D])
        XN = sb("XN", [P, NT, D])
        HT = sb("HT", [P, 2, NP])
        ADJ = sb("ADJ", [P, SLOTS, NP])
        P01 = sb("P01", [P, NT, D])
        Y = sb("Y", [P, NT, H])
        stage = sb("stage", [P, SLOTS, D])
        p01 = P01[:, :, :].rearrange("p t d -> p (t d)")
        src_i = p01[0:EP, 0:ET].bitcast(I32)
        dst_i = p01[0:EP, ET:2 * ET].bitcast(I32)
        val = p01[0:EP, 2 * ET:3 * ET]
        srcf = p01[0:EP, 3 * ET:4 * ET]
        dstf = p01[0:EP, 4 * ET:5 * ET]
        quo = p01[0:EP, 5 * ET:6 * ET]
        key = p01[0:EP, 6 * ET:6 * ET + ET + 2]
        pos_all = p01[0:EP, 7 * ET + 2:8 * ET + 2]
        rec = p01[0:EP, 8 * ET + 2:12 * ET + 2].rearrange("p (t f) -> p t f", f=4)
        yf = Y[:, :, :].rearrange("p t d -> p (t d)")
        recL = yf[:, 0:NG * 4].rearrange("p (g f) -> p g f", f=4)
        adjf = ADJ[:, :, :].rearrange("p s n -> p (s n)")
        oh = adjf[0:EP, 0:5 * 320].bitcast(BF16).rearrange("p (s n) -> p s n", s=5)
        junk = adjf[0:EP, 1600:1600 + 5 * 320].bitcast(BF16).rearrange("p (s n) -> p s n", s=5)
        zeros = adjf[:, 3200:3200 + NG * 4]
        iota_i = adjf[:, 6400:6400 + 640].bitcast(I32)
        iota_g = sb("iota_g", [P, 640], F16)
        iota_n = sb("iota_n", [P, P])
        ones_f = sb("ones_f", [P, P])
        ident = sb("ident", [P, P])
        before_f = sb("before_f", [P, P])
        before = sb("before", [P, P], BF16)
        upto = sb("upto", [P, P])
        notbefore = sb("notbefore", [P, P], BF16)
        ones_b = sb("ones_b", [P, P], BF16)
        pos5 = sb("pos5", [EP, 2, B5])
        idx5 = sb("idx5", [EP, 2, B5], I32)
        rec5 = sb("rec5", [EP, 2, B5, 4])
        dummy = sb("carrier", [P, 4])
        work = sb("work", [P, SLOTS, D])
        ohc = work[:, :, 0:P]
        ohr = work[:, :, P:2 * P]
        idx_all = dst_i
        big_all = srcf
        low_all = dstf
        pmax = sb("pmax", [EP, 1])
        prow = sb("prow", [1, P])
        rounds = sb("rounds", [1, 1], I32)
        htf = HT[:, :, :].rearrange("p c n -> p (c n)")
        wk_n = htf[:, 0:512].rearrange("p (r n) -> p r n", r=2)
        wv_n = htf[:, 512:1024].rearrange("p (r n) -> p r n", r=2)
        wo_n = htf[:, 1024:1536].rearrange("p (r n) -> p r n", r=2)
        W0_n = htf[:, 1536:1792]
        W1_n = htf[:, 1792:1920]
        b1_n = htf[0:NE, 1920:2944]
        wkvT = htf[:, 2944:3968].rearrange("p (c n) -> p c n", c=2)
        wq_n = p01[:, 5104:5616].rearrange("p (r n) -> p r n", r=2)
        woT = p01[:, 5616:6128].rearrange("p (r n) -> p r n", r=2)
        W0T = sb("W0T", [P, 2, H])
        W1T = sb("W1T", [P, H])
        b1T = sb("b1T", [P, F // P, NE])
        gate_w = sb("gate_w", [P, 2, NE])
        rows = sb("rows", [1, 2 * D + NE + 2 * D])
        bo_r = rows[:, 0:D]
        gb1_r = rows[:, D:D + H]
        gate_b = rows[:, D + H:D + H + NE]
        vg_r = rows[:, 2 * D + NE:2 * D + NE + HD]
        vb_r = rows[:, 2 * D + NE + HD:2 * D + NE + 2 * HD]
        cols = sb("cols", [P, 4])
        gvb = sb("gvb", [P, 2, HD])
        hm = sb("hm", [P, 2, NH])
        KC = adjf[:, 0:NT * 512].rearrange("p (t n) -> p t n", t=NT)
        sq = adjf[:, NT * 512:NT * 512 + SLOTS * 512].rearrange("p (s n) -> p s n", s=SLOTS)
        hvar = sb("hvar", [P, NT * NH])
        hrs = sb("hrs", [P, NT * NH])
        hta = adjf[:, NT * 512 + SLOTS * 512:NT * 512 + SLOTS * 512 + NT * NH]
        khat = sq
        kvp = sb("kvp", [P, 2, P])
        kvc = sb("kvc", [P, 2, 4])
        M = sb("M", [P, 2, D])
        bc = [HT[:, k, :].rearrange("p (g n) -> p g n", g=NR) for k in range(2)]
        br = [ADJ[:, 2 + k, :].rearrange("p (g n) -> p g n", g=NR) for k in range(2)]
        nmx = sb("nmx", [P, SLOTS])
        rsum = sb("rsum", [P, SLOTS])
        rrec = sb("rrec", [P, SLOTS])
        LG = yf[:, 0:NT * NE].rearrange("p (t e) -> p t e", e=NE)
        OH8 = yf[:, NT * NE:2 * NT * NE].rearrange("p (t e) -> p t e", e=NE)
        ta8 = kvp[:, :, :].rearrange("p a b -> p (a b)")[:, 0:NT * NE].rearrange("p (t e) -> p t e", e=NE)
        tb8 = M[:, 0, 0:NT * NE].rearrange("p (t e) -> p t e", e=NE)
        tc8 = M[:, 1, 0:NT * NE].rearrange("p (t e) -> p t e", e=NE)
        rt = yf[:, 2 * NT * NE:3 * NT * NE].rearrange("p (a t) -> p a t", t=NT)
        sidx = sb("sidx", [P, NT], I32)
        gidx = sb("gidx", [P, NT], I32)
        kp = sb("kp", [P, NT])
        w1s = adjf[:, 0:4096].rearrange("p (s c f) -> p s c f", s=2, c=2)
        w2s = adjf[:, 4096:8192].rearrange("p (s c f) -> p s c f", s=2, c=8)
        xbs = adjf[:, 8192:10240].rearrange("p (s c f) -> p s c f", s=2, c=4)
        xbT = adjf[:, 10240:12288].rearrange("p (s c f) -> p s c f", s=2, c=2)
        b2_b = adjf[:, 12288:12288 + NE * D]
        hmT = htf[:, 0:4096].rearrange("p (c f) -> p c f", c=8)
        ybs = htf[:, 4096:6144].rearrange("p (s c f) -> p s c f", s=2, c=4)
        G = P01
        big = sb("big", [P, 1])
        nbig = sb("nbig", [P, 1])
        zpad = sb("zpad", [P, 1])
        sums = sb("sums", [P, NT])
        check = sb("check", [P, 1])
        odd = sb("odd", [1, 1], I32)
        nanm = work[:, 0:2, :].bitcast(I32)
        bst = sb("bst", [P, NT, 6])
        lnm = sb("lnm", [P, NT])
        lnr = sb("lnr", [P, NT])
        lna = sb("lna", [P, NT])
        lnb = sb("lnb", [P, NT])

        ps = ctx.enter_context(nc.psum_tensor("ps", [P, 8, 512], F32))

        s_edge = sem("s_edge")
        s_x = sem("s_x")
        s_zero = sem("s_zero")
        s_recz = sem("s_recz")
        s_const = sem("s_const")
        s_constv = sem("s_constv")
        s_dve = sem("s_dve")
        s_oh = sem("s_oh")
        s_rank = sem("s_rank")
        s_rankrd = sem("s_rankrd")
        s_idx = sem("s_idx")
        s_rec = sem("s_rec")
        s_prep = sem("s_prep")
        s_scat = [sem(f"s_scat{i}") for i in range(2)]
        s_recl = sem("s_recl")
        s_hot = sem("s_hot")
        s_wgt = sem("s_wgt")
        s_tail = sem("s_tail")
        s_bmm = sem("s_bmm")
        s_bev = sem("s_bev")
        s_ast = [sem(f"s_ast{i}") for i in range(2)]
        s_ald = [sem(f"s_ald{i}") for i in range(SLOTS)]
        s_stage = sem("s_stage")
        s_xn = sem("s_xn")
        s_stats = sem("s_stats")
        s_var = sem("s_var")
        s_root = sem("s_root")
        s_carry = sem("s_carry")
        s_tile = sem("s_tile")
        s_acc = sem("s_acc")
        s_w = sem("s_w")
        s_wt = sem("s_wt")
        s_wtv = sem("s_wtv")
        s_xz = sem("s_xz")
        phase = {}
        for tag, steps in (("mixa", "turned xt prod"), ("mixb", "turned xt prod read"), ("gate", "turned xt prod read"),
                           ("hn", "turned read"), ("sm0", "turned"), ("sm1", "turned")):
            for what in steps.split():
                phase[tag, what] = sem(f"{tag}_{what}")
        s_sq = sem("s_sq")
        s_hred = sem("s_hred")
        s_hvar = sem("s_hvar")
        s_hroot = sem("s_hroot")
        s_khat = sem("s_khat")
        s_kvt = sem("s_kvt")
        s_kvp = sem("s_kvp")
        s_t1 = sem("s_t1")
        s_t1v = sem("s_t1v")
        s_m = sem("s_m")
        s_mv = sem("s_mv")
        s_z = {l: sem(f"s_z{l}") for l in (0, 1)}
        s_zt = {l: sem(f"s_zt{l}") for l in (0, 1)}
        s_nm = {l: sem(f"s_nm{l}") for l in (0, 1)}
        s_ex = {l: sem(f"s_ex{l}") for l in (0, 1)}
        s_rr = {l: sem(f"s_rr{l}") for l in (0, 1)}
        s_sm = {l: sem(f"s_sm{l}") for l in (0, 1)}
        s_sum = [sem(f"s_sum{l}") for l in (0, 1)]
        s_tanh = [sem(f"s_tanh{l}") for l in (0, 1)]
        s_x1h = sem("s_x1h")
        s_x1 = sem("s_x1")
        s_xn2 = sem("s_xn2")
        s_exp8 = sem("s_exp8")
        s_one8 = sem("s_one8")
        s_cnt = sem("s_cnt")
        s_slot = sem("s_slot")
        s_disp = sem("s_disp")
        s_b2 = sem("s_b2")
        s_wl = [sem(f"s_wl{i}") for i in range(2)]
        s_xbt = sem("s_xbt")
        s_xbv = sem("s_xbv")
        s_hid = sem("s_hid")
        s_hidv = sem("s_hidv")
        s_y = sem("s_y")
        s_yv = sem("s_yv")
        s_yst = [sem(f"s_yst{i}") for i in range(2)]
        s_gat = [sem(f"s_gat{j}") for j in range(NT)]
        s_max = sem("s_max")
        s_rounds = sem("s_rounds")
        m_dve = sem("m_dve")
        m_carry = sem("m_carry")
        m_own = sem("m_own")
        m_copy = sem("m_copy")
        m_idx = sem("m_idx")
        m_zero = sem("m_zero")
        m_clear = sem("m_clear")
        m_scat = sem("m_scat")
        m_recl = sem("m_recl")
        m_load = sem("m_load")
        m_store = sem("m_store")
        m_pair = sem("m_pair")
        m_mm = sem("m_mm")
        m_add = sem("m_add")
        s_fin = sem("s_fin")
        s_check = sem("s_check")
        s_odd = sem("s_odd")
        s_fixed = sem("s_fixed")
        s_again = sem("s_again")
        s_out = sem("s_out")

        @contextmanager
        def more_rounds(eng):
            count = eng.value_load(rounds[0:1, 0:1], min_val=1, max_val=E // CAP + 1)
            with eng.If(count > 1):
                with eng.Fori(1, count) as k:
                    yield k

        block = ctx.enter_context(nc.Block())

        @block.sync
        def _(sp):
            sp.dma_start(src_i, a["src"].rearrange("(p t) -> p t", t=ET)).then_inc(s_edge, 16)
            sp.dma_start(dst_i, a["dst"].rearrange("(p t) -> p t", t=ET)).then_inc(s_edge, 16)
            sp.dma_start(val, a["edge_weight"].rearrange("(p t) -> p t", t=ET)).then_inc(s_edge, 16)
            row = lambda name: a[name].rearrange("(a n) -> a n", a=1)
            half = lambda name: a[name].rearrange("(r p) n -> p r n", p=P)
            for dst, src in ((wk_n, half("L0_mix_wk")), (wv_n, half("L0_mix_wv")), (wo_n, half("L0_mix_wo")), (wq_n[:, :, :], half("L0_mix_wq")),
                             (W0_n, a["L0_gnn_W0"]), (W1_n, a["L0_gnn_W1"]), (b1_n, a["L0_ffn_b1"]), (gate_w[:, :, :], half("L0_ffn_gate_w")),
                             (bo_r, row("L0_mix_bo")), (gb1_r, row("L0_gnn_b1")), (gate_b, row("L0_ffn_gate_b")),
                             (vg_r, row("L0_mix_ln_v_g")), (vb_r, row("L0_mix_ln_v_b")),
                             (cols[:, 0:1], a["L0_gnn_b0"].rearrange("(p a) -> p a", a=1)),
                             (cols[0:HD, 1:2], a["L0_mix_ln_k_g"].rearrange("(p a) -> p a", a=1)),
                             (cols[HD:P, 1:2], a["L0_mix_ln_k_g"].rearrange("(p a) -> p a", a=1)),
                             (cols[0:HD, 2:3], a["L0_mix_ln_k_b"].rearrange("(p a) -> p a", a=1)),
                             (cols[HD:P, 2:3], a["L0_mix_ln_k_b"].rearrange("(p a) -> p a", a=1))):
                sp.dma_start(dst, src).then_inc(s_w, 16)
            sp.wait_ge(s_zero, 3)
            sp.dma_start(rec_dram.rearrange("(s g) f -> s (g f)", g=NG), zeros).then_inc(s_recz, 16)
            sp.dma_start(X1[:, 0:NT - 1, :], a["x"][0:(NT - 1) * P, :].rearrange("(j p) d -> p j d", p=P)).then_inc(s_x, 16)
            sp.wait_ge(s_const, 6)
            sp.dma_start(X1[0:LAST, NT - 1, :], a["x"][(NT - 1) * P:N, :]).then_inc(s_x, 16)
            for i in range(4):
                sp.dma_start(xbuf_dram.rearrange("(p c) d -> p (c d)", p=P)[:, i * 2048:(i + 1) * 2048], zeros[:, 0:2048]).then_inc(s_xz, 16)
            sp.wait_ge(s_scat[0], 16 * B5 * ((NB + 1) // 2))
            sp.wait_ge(s_scat[1], 16 * B5 * (NB // 2))
            sp.dma_start(recL.rearrange("p g f -> p (g f)"), rec_dram.rearrange("(s g) f -> s (g f)", g=NG)).then_inc(s_recl, 16)
            def store(j, slot):
                sp.wait_ge(s_bev, 7 * (j + 1))
                sp.dma_start(adj_dram[ds(j, 1), :, :].rearrange("a p n -> p (a n)"), ADJ[:, slot, :]).then_inc(s_ast[slot], 16)
            with sp.Fori(0, NT // 2) as i:
                store(i * 2, 0)
                store(i * 2 + 1, 1)
            store(NT - 1, 0)
            sp.wait_ge(s_ast[0], 16 * (NT // 2 + 1))
            sp.wait_ge(s_ast[1], 16 * (NT // 2))
            sp.wait_ge(s_rounds, 1)
            with more_rounds(sp) as k:
                sp.wait_ge(m_zero, k)
                sp.dma_start(rec_dram.rearrange("(s g) f -> s (g f)", g=NG), zeros).then_inc(m_clear, 16)
                sp.wait_ge(m_scat, 16 * ET)
                sp.dma_start(recL.rearrange("p g f -> p (g f)"), rec_dram.rearrange("(s g) f -> s (g f)", g=NG)).then_inc(m_recl, 16)
                with sp.Fori(0, NT) as j:
                    tile = k * NT + j - NT
                    sp.dma_start(ADJ[:, 0, :], adj_dram[ds(j, 1), :, :].rearrange("a p n -> p (a n)")).then_inc(m_load, 16)
                    sp.wait_ge(m_add, tile * NR + NR)
                    sp.dma_start(adj_dram[ds(j, 1), :, :].rearrange("a p n -> p (a n)"), ADJ[:, 0, :]).then_inc(m_store, 16)
                    sp.wait_ge(m_store, tile * 16 + 16)
                    sp.sem_inc(m_carry, 1)
            for half in range(2):
                def load(j, slot, first):
                    if not (first and half == 0):
                        sp.wait_ge(s_tile, half * NT + j - SLOTS + 1)
                    sp.dma_start(ADJ[:, slot, 0:4 * CHUNK],
                                 adj_dram[ds(j, 1), :, half * 4 * CHUNK:(half + 1) * 4 * CHUNK].rearrange("a p n -> p (a n)")).then_inc(s_ald[slot], 16)
                for j in range(SLOTS):
                    load(j, j, True)
                with sp.Fori(1, NT // SLOTS) as i:
                    for j in range(SLOTS):
                        load(i * SLOTS + j, j, False)
            for l in (0, 1):
                def load(j, slot):
                    if l == 0:
                        if isinstance(j, int):
                            sp.wait_ge(s_tile, 2 * NT - SLOTS + 1 + j)
                        else:
                            sp.wait_ge(s_zt[0], j - SLOTS + 1)
                    else:
                        if isinstance(j, int):
                            sp.wait_ge(s_zt[0], NT - SLOTS + 1 + j)
                        else:
                            sp.wait_ge(s_zt[1], j - SLOTS + 1)
                    sp.dma_start(ADJ[:, slot, 0:8 * CHUNK], adj_dram[ds(j, 1), :, 0:8 * CHUNK].rearrange("a p n -> p (a n)")).then_inc(s_ald[slot], 16)
                tiles(sp, load)
            sp.wait_ge(s_zt[1], NT)
            sp.dma_start(b2_b, a["L0_ffn_b2"].rearrange("e d -> (e d)").partition_broadcast(P)).then_inc(s_b2, 16)

            def weights(e, s):
                sp.dma_start(w1s[:, s, :, :], a["L0_ffn_w1"][ds(e, 1), :, :].rearrange("a (c p) f -> p (a c) f", p=P)).then_inc(s_wl[s], 16)
                sp.dma_start(w2s[:, s, :, :], a["L0_ffn_w2"][ds(e, 1), :, :].rearrange("a (c p) f -> p (a c) f", p=P)).then_inc(s_wl[s], 16)

            def tokens(e, s):
                sp.dma_start(xbs[:, s, :, :], xbuf_dram[ds(e * XS, XS), :].rearrange("(c p) f -> p c f", p=P)).then_inc(s_wl[s], 16)

            def ystore(e, s):
                sp.wait_ge(s_yv, 4 * (e + 1))
                sp.dma_start(ybuf_dram[ds(e * XS, XS), :].rearrange("(c p) f -> p c f", p=P), ybs[:, s, :, :]).then_inc(s_yst[s], 16)
            weights(0, 0)
            weights(1, 1)
            sp.wait_ge(s_disp, 16 * NT)
            tokens(0, 0)
            tokens(1, 1)
            with sp.Fori(0, NE // 2 - 1) as i:
                for s in range(2):
                    ystore(i * 2 + s, s)
                    weights(i * 2 + s + 2, s)
                    tokens(i * 2 + s + 2, s)
            for s in range(2):
                ystore(NE - 2 + s, s)
            for j in range(NT):
                sp.wait_ge(s_fin, j + 1)
                n = P if j < NT - 1 else LAST
                sp.dma_start(out[j * P:j * P + n, :], XN[0:n, j, :]).then_inc(s_out, 16)
            sp.wait_ge(s_odd, 1)
            with sp.If(sp.value_load(odd[0:1, 0:1], min_val=0, max_val=1) > 0):
                for j in range(NT):
                    n = P if j < NT - 1 else LAST
                    sp.wait_ge(s_fixed, j + 1)
                    sp.dma_start(out[j * P:j * P + n, :], XN[0:n, j, :]).then_inc(s_again, 16)
                sp.wait_ge(s_again, 16 * NT)
            sp.wait_ge(s_out, 16 * NT)

        @block.gpsimd
        def _(gp):
            gp.memset(zeros, 0.0).then_inc(s_zero, 1)
            gp.memset(adjf[0:EP, 0:1600], 0.0).then_inc(s_zero, 1)
            gp.memset(dummy[:, :], 0.0).then_inc(s_zero, 1)
            gp.iota(iota_i, pattern=[[1, 640]], base=0, channel_multiplier=0).then_inc(s_const, 1)
            gp.memset(ones_f[:, :], 1.0).then_inc(s_const, 1)
            gp.wait_ge(s_const, 2)
            gp.affine_select(out=before_f[:, :], in_=ones_f[:, :], compare_op=ALU.is_gt, fill=0.0,
                             base=0, pattern=[[1, P]], channel_multiplier=-1).then_inc(s_const, 1)
            gp.affine_select(out=ident[:, :], in_=ones_f[:, :], compare_op=ALU.is_equal, fill=0.0,
                             base=0, pattern=[[1, P]], channel_multiplier=-1).then_inc(s_const, 1)
            gp.affine_select(out=upto[:, :], in_=ones_f[:, :], compare_op=ALU.is_ge, fill=0.0,
                             base=0, pattern=[[1, P]], channel_multiplier=-1).then_inc(s_const, 1)
            gp.memset(X1[:, NT - 1, :], 0.0).then_inc(s_const, 1)
            gp.wait_ge(s_recz, 16)
            gp.wait_ge(s_zero, 3)

            def scatter(b, q):
                gp.wait_ge(s_idx, b + 1)
                gp.wait_ge(s_rec, b + 1)
                if not isinstance(b, int):
                    gp.wait_ge(s_carry, b)
                gp.tensor_tensor(dummy[:, 0:1], dummy[:, 1:2], dummy[:, 2:3], ALU.add).then_inc(s_carry, 1)
                for i in range(B5):
                    gp.indirect_dma_start(rec_dram[:, :], bass.IndirectOffsetOnAxis(ap=idx5[:, q, i:i + 1], axis=0),
                                          rec5[:, q, i, :], None, bounds_check=CAP * NG - 1, oob_is_err=False).then_inc(s_scat[q], 16)
            scatter(0, 0)
            with gp.Fori(0, NB // 2) as m:
                scatter(m * 2 + 1, 1)
                scatter(m * 2 + 2, 0)

            gp.wait_ge(s_ast[0], 16 * (NT // 2 + 1))
            gp.wait_ge(s_ast[1], 16 * (NT // 2))
            gp.wait_ge(s_rounds, 1)
            with more_rounds(gp) as k:
                gp.wait_ge(m_idx, k)
                gp.sem_inc(m_carry, 1)
                gp.memset(zeros, 0.0).then_inc(m_zero, 1)
                gp.wait_ge(m_clear, k * 16)
                gp.sem_inc(m_carry, 1)
                with gp.Fori(0, NB) as b:
                    batch = k * NB + b - NB
                    gp.tensor_copy(idx5[:, 0, :], idx_all[:, ds(b * B5, B5)]).then_inc(m_copy, 1)
                    gp.tensor_copy(rec5[:, 0, :, :], rec[:, ds(b * B5, B5), :]).then_inc(m_copy, 1)
                    gp.wait_ge(m_copy, batch * 2 + 2)
                    gp.tensor_tensor(dummy[:, 0:1], dummy[:, 1:2], dummy[:, 2:3], ALU.add).then_inc(m_own, 1)
                    for i in range(B5):
                        gp.indirect_dma_start(rec_dram[:, :], bass.IndirectOffsetOnAxis(ap=idx5[:, 0, i:i + 1], axis=0),
                                              rec5[:, 0, i, :], None, bounds_check=CAP * NG - 1, oob_is_err=False).then_inc(m_scat, 16)
                    gp.wait_ge(m_scat, b * (16 * B5) + 16 * B5)
                    gp.wait_ge(m_own, batch + 1)
                gp.wait_ge(m_recl, k * 16)
                gp.sem_inc(m_carry, 1)
                gp.inc_swdge_sem([m_scat], [16 * ET], mode="sub")
            gp.wait_ge(s_slot, 1)
            gp.wait_ge(s_xz, 64)
            for j in range(NT):
                n = P if j < NT - 1 else LAST
                gp.indirect_dma_start(xbuf_dram[:, :], bass.IndirectOffsetOnAxis(ap=sidx[0:n, j:j + 1], axis=0),
                                      XN[0:n, j, :], None, bounds_check=NE * XS - 1, oob_is_err=False).then_inc(s_disp, 16)
            for s in range(2):
                gp.wait_ge(s_yst[s], 16 * NE // 2)
            for j in range(NT):
                n = P if j < NT - 1 else LAST
                gp.indirect_dma_start(G[0:n, j, :], None, ybuf_dram[:, :],
                                      bass.IndirectOffsetOnAxis(ap=gidx[0:n, j:j + 1], axis=0)).then_inc(s_gat[j], 16)

        @block.scalar
        def _(act):
            act.wait_ge(s_prep, 1)

            def batch(b, q, first):
                if not first:
                    act.wait_ge(s_scat[q], 16 * B5 * ((b - q) // 2) if isinstance(b, int) else first_wait(b, q))
                nc.scalar.copy(rec5[:, q, :, :], rec[:, ds(b * B5, B5), :]).then_inc(s_rec, 1)
            batch(0, 0, True)
            batch(1, 1, True)
            batch(2, 0, False)
            with act.Fori(1, NB // 2) as m:
                for k, q in ((1, 1), (2, 0)):
                    act.wait_ge(s_scat[q], (m + (1 if q == 0 else 0)) * (16 * B5))
                    nc.scalar.copy(rec5[:, q, :, :], rec[:, ds((m * 2 + k) * B5, B5), :]).then_inc(s_rec, 1)

            act.wait_ge(s_var, 1)
            nc.scalar.activation(lnr[:, :], lnb[:, :], ACT.Sqrt).then_inc(s_root, 1)

            def kv(j, s):
                act.wait_ge(phase["mixa", "prod"], j + 1)
                bank = ps[:, 5 + s % 3, :]
                nc.scalar.copy(KC[:, ds(j, 1), :].rearrange("p a d -> p (a d)"), bank)
                ge(act, s_hred, j - SLOTS + 1)
                nc.scalar.activation(sq[:, s, :], bank, ACT.Square).then_inc(s_sq, 1)
            act.wait_ge(s_recz, 16)
            act.wait_ge(s_xz, 64)
            tiles(act, kv)
            act.wait_ge(s_hvar, 1)
            nc.scalar.activation(hrs[:, :], hvar[:, :], ACT.Sqrt).then_inc(s_hroot, 1)

            def weigh(j, k, c):
                g0, g1 = PARTS[c][0:2]
                act.wait_ge(s_hot, (j * len(PARTS) + c) * 2 + 1)
                act.sem_inc(m_carry, 1)
                for g in range(g0 + DW, g1):
                    nc.scalar.activation(bc[k][:, g, :], bc[k][:, g, :], ACT.Copy, scale=recL[:, ds(j * NR + g, 1), 2]).then_inc(s_wgt, 1)

            def evac(j, slot, c, first):
                if c == 0 and not first:
                    act.wait_ge(s_ast[slot], (j - slot) * 8)
                for q in range(*PARTS[c][2:4]):
                    w = min(4, NR - 4 * q)
                    act.wait_ge(s_bmm, j * NR + 4 * q + w)
                    dst = ADJ[:, slot, :].rearrange("p (r g) -> p r g", g=NR)[:, :, 4 * q:4 * q + w]
                    nc.scalar.copy(dst, ps[:, q, 0:w * P].rearrange("p (g r) -> p r g", r=P)).then_inc(s_bev, 1)

            def both(j, slot, first):
                for c in range(len(PARTS)):
                    if not (isinstance(j, int) and j == NT - 1):
                        weigh(j + 1, 1 - slot, c)
                    evac(j, slot, c, first)
            for c in range(len(PARTS)):
                weigh(0, 0, c)
            both(0, 0, True)
            both(1, 1, True)
            with act.Fori(1, NT // 2) as i:
                both(i * 2, 0, False)
                both(i * 2 + 1, 1, False)
            both(NT - 1, 0, False)

            act.wait_ge(s_xn, NT)
            for half in range(2):
                def st(j, slot, first):
                    if not (first and half == 0):
                        act.wait_ge(s_tile, half * NT + j - SLOTS + 1)
                    nc.scalar.copy(stage[:, slot, :], XN[:, ds(j, 1), :].rearrange("p a d -> p (a d)")).then_inc(s_stage, 1)
                for j in range(SLOTS):
                    st(j, j, True)
                with act.Fori(1, NT // SLOTS) as i:
                    for j in range(SLOTS):
                        st(i * SLOTS + j, j, False)
                act.wait_ge(s_tile, (half + 1) * NT)
                for dd in range(2):
                    for q in range(4):
                        c = (half * 4 + q) * CHUNK
                        nc.scalar.copy(HT[:, dd, c:c + CHUNK], ps[:, dd * 4 + q, 0:CHUNK]).then_inc(s_acc, 1)

            def tanh(l):
                def step(j, s):
                    act.wait_ge(s_sum[l], j + 1)
                    t = P01[:, ds(j, 1), l * H:(l + 1) * H].rearrange("p a d -> p (a d)")
                    nc.scalar.activation(t, t, ACT.Tanh).then_inc(s_tanh[l], 1)
                return step

            def tanh0(j, s):
                act.wait_ge(s_sum[0], j + 1)
                nc.scalar.activation(work[:, s, 0:H], work[:, s, 0:H], ACT.Tanh).then_inc(s_tanh[0], 1)

            for l in (0, 1):
                def st(j, s):
                    if l == 0:
                        if isinstance(j, int):
                            act.wait_ge(phase["hn", "turned"], NT)
                            act.wait_ge(phase["hn", "read"], NT)
                        else:
                            act.wait_ge(s_zt[0], j - SLOTS + 1)
                        nc.scalar.copy(stage[:, s, 0:H], Y[:, ds(j, 1), :].rearrange("p a d -> p (a d)")).then_inc(s_stage, 1)
                    else:
                        if isinstance(j, int):
                            act.wait_ge(phase["sm0", "turned"], NT)
                            act.wait_ge(s_sm[0], NT)
                        else:
                            act.wait_ge(s_zt[1], j - SLOTS + 1)
                        nc.scalar.copy(stage[:, s, 0:H], P01[:, ds(j, 1), 0:H].rearrange("p a d -> p (a d)")).then_inc(s_stage, 1)
                for j in range(SLOTS):
                    st(j, j)
                if l == 1:
                    tiles(act, tanh0)
                with act.Fori(1, NT // SLOTS) as i:
                    for j in range(SLOTS):
                        st(i * SLOTS + j, j)
                act.wait_ge(s_zt[l], NT)
                for q in range(8):
                    c = q * CHUNK
                    if l == 0:
                        nc.scalar.activation(HT[:, 0, c:c + CHUNK], ps[:, q, 0:CHUNK], ACT.Identity, bias=cols[:, 0:1]).then_inc(s_z[l], 1)
                    else:
                        nc.scalar.copy(HT[:, 0, c:c + CHUNK], ps[:, q, 0:CHUNK]).then_inc(s_z[l], 1)

                def ex(j, s):
                    act.wait_ge(s_nm[l], j + 1)
                    ge(act, s_sm[0] if l == 0 else s_sum[1], j - SLOTS + 1)
                    nc.scalar.activation(work[:, s, 0:H], ps[:, s % 3, 0:H], ACT.Exp, bias=nmx[:, s:s + 1],
                                         accum_out=rsum[:, s:s + 1]).then_inc(s_ex[l], 1)
                if l == 0:
                    tiles(act, ex)
                else:
                    tiles_ahead(act, ex, tanh(1))
            act.wait_ge(s_var, 2)
            nc.scalar.activation(lnr[:, :], lnb[:, :], ACT.Sqrt).then_inc(s_root, 1)
            act.wait_ge(s_exp8, 1)
            nc.scalar.activation(ta8, tb8, ACT.Exp).then_inc(s_exp8, 1)

            def rows_out(e, s):
                for c in range(2):
                    act.wait_ge(s_xbt, 2 * e + c + 1)
                    nc.scalar.copy(xbT[:, s, c, :], ps[:, c, :]).then_inc(s_xbv, 1)

            def hidden(e):
                for f in range(8):
                    act.wait_ge(s_hid, 8 * e + f + 1)
                    if f == 0:
                        ge(act, s_y, 4 * e)
                    nc.scalar.activation(hmT[:, f, 0:CAPX], ps[:, 2 + f % 3, 0:CAPX], ACT.Relu, bias=b1T[:, f, ds(e, 1)]).then_inc(s_hidv, 1)
            rows_out(0, 0)
            hidden(0)
            rows_out(1, 1)
            with act.Fori(1, NE // 2) as i:
                hidden(i * 2 - 1)
                rows_out(i * 2, 0)
                hidden(i * 2)
                rows_out(i * 2 + 1, 1)
            hidden(NE - 1)

        @block.vector
        def _(dve):
            v = nc.vector
            chain = [0]

            def link(ins):
                chain[0] += 1
                ins.then_inc(s_dve, 1)
                dve.wait_ge(s_dve, chain[0])

            def norm_scale(n):
                me, se, mo, so = bst[:, :, 1], bst[:, :, 2], bst[:, :, 4], bst[:, :, 5]
                link(v.tensor_tensor(lnm[:, :], me, mo, ALU.add))
                link(v.tensor_scalar(lnm[:, :], lnm[:, :], 0.5, None, ALU.mult))
                link(v.tensor_tensor(lna[:, :], me, mo, ALU.subtract))
                link(v.scalar_tensor_tensor(out=lna[:, :], in0=lna[:, :], scalar=0.25, in1=lna[:, :], op0=ALU.mult, op1=ALU.mult))
                link(v.tensor_tensor(lnb[:, :], se, so, ALU.add))
                link(v.scalar_tensor_tensor(out=lnb[:, :], in0=lnb[:, :], scalar=1.0 / D, in1=lna[:, :], op0=ALU.mult, op1=ALU.add))
                v.tensor_scalar(lnb[:, :], lnb[:, :], EPS, None, ALU.add).then_inc(s_var, 1)
                dve.wait_ge(s_root, n + 1)
                link(v.reciprocal(lna[:, :], lnr[:, :]))
                link(v.tensor_tensor(lna[:, :], lna[:, :], lnb[:, :], ALU.mult))
                link(v.tensor_tensor(lnr[:, :], lnr[:, :], lna[:, :], ALU.add))
                link(v.tensor_scalar(lnr[:, :], lnr[:, :], 0.5, None, ALU.mult))
                link(v.reciprocal(lnr[:, :], lnr[:, :]))

            dve.wait_ge(s_edge, 48)
            v.tensor_copy(srcf, src_i).then_inc(s_dve, 1)
            link_base = chain[0]
            chain[0] += 1
            link(v.tensor_copy(dstf, dst_i))
            link(v.tensor_scalar(quo, dstf, 1.0 / P, 0.5 / P - 0.5, ALU.mult, ALU.add))
            link(v.tensor_scalar(quo, quo, MAGIC, MAGIC, ALU.add, ALU.subtract))
            link(v.scalar_tensor_tensor(out=rec[:, :, 0], in0=quo, scalar=-float(P), in1=dstf, op0=ALU.mult, op1=ALU.add))
            link(v.tensor_scalar(key[:, 0:ET], quo, float(NR), None, ALU.mult))
            link(v.tensor_scalar(quo, srcf, 1.0 / NR, 0.5 / NR - 0.5, ALU.mult, ALU.add))
            link(v.tensor_scalar(rec[:, :, 1], quo, MAGIC, MAGIC, ALU.add, ALU.subtract))
            link(v.scalar_tensor_tensor(out=quo, in0=rec[:, :, 1], scalar=-float(NR), in1=srcf, op0=ALU.mult, op1=ALU.add))
            link(v.tensor_tensor(key[:, 0:ET], key[:, 0:ET], quo, ALU.add))
            link(v.memset(key[:, ET:ET + 2], -1.0))
            link(v.tensor_copy(rec[:, :, 2], val))
            v.memset(rec[:, :, 3], 0.0).then_inc(s_prep, 1)
            dve.wait_ge(s_const, 6)
            link(v.tensor_copy(iota_g[:, :], iota_i))
            link(v.tensor_copy(iota_n[:, :], iota_i[:, 0:P]))
            link(v.tensor_copy(before[:, :], before_f[:, :]))
            link(v.tensor_scalar(notbefore[:, :], before_f[:, :], -1.0, 1.0, ALU.mult, ALU.add))
            v.tensor_copy(ones_b[:, :], ones_f[:, :]).then_inc(s_constv, 1)
            dve.wait_ge(s_zero, 3)

            def onehot(t, slot):
                v.tensor_scalar(oh[:, slot, 0:NG], iota_g[0:EP, 0:NG], key[:, ds(t, 1)], None, ALU.is_equal).then_inc(s_oh, 1)

            def rank(t, i, par, q):
                dve.wait_ge(s_rank, t + 1)
                v.tensor_tensor_reduce(out=junk[:, i % 5, 0:NG], in0=ps[0:EP, 2 * par:2 * par + 2, :].rearrange("p b n -> p (b n)")[:, 0:NG],
                                       in1=oh[:, i % 5, 0:NG], scale=1.0, scalar=0.0, op0=ALU.mult, op1=ALU.add,
                                       accum_out=pos5[:, q, i % 5:i % 5 + 1]).then_inc(s_rankrd, 1)
                onehot(t + 2, (i + 2) % 5)

            def slots(b, q, wait):
                if wait is not None:
                    dve.wait_ge(s_scat[q], wait)
                dve.wait_ge(s_rankrd, (b + 1) * B5)
                v.scalar_tensor_tensor(out=idx5[:, q, :], in0=pos5[:, q, :], scalar=float(NG),
                                       in1=key[:, ds(b * B5, B5)], op0=ALU.mult, op1=ALU.add).then_inc(s_idx, 1)
                v.tensor_copy(pos_all[:, ds(b * B5, B5)], pos5[:, q, :])

            onehot(0, 0)
            onehot(1, 1)
            for i in range(B5):
                rank(i, i, i % 2, 0)
            slots(0, 0, None)
            for i in range(B5):
                rank(B5 + i, i, (i + 1) % 2, 1)
            slots(1, 1, None)
            for i in range(B5):
                rank(2 * B5 + i, i, i % 2, 0)
            slots(2, 0, 16 * B5)
            with dve.Fori(1, NB // 2) as m:
                for i in range(B5):
                    rank(m * 10 + 5 + i, i, (1 + i) % 2, 1)
                slots(m * 2 + 1, 1, m * (16 * B5))
                for i in range(B5):
                    rank(m * 10 + 10 + i, i, i % 2, 0)
                slots(m * 2 + 2, 0, (m + 1) * (16 * B5))

            dve.wait_ge(s_rankrd, ET)
            link(v.engine_nop())
            v.tensor_reduce(pmax[:, :], pos_all, AX_X, ALU.max).then_inc(s_max, 1)
            dve.wait_ge(s_max, 2)
            link(v.tensor_reduce(prow[:, 0:1], ps[0:1, 7, 0:EP], AX_X, ALU.max))
            link(v.tensor_scalar(prow[:, 0:1], prow[:, 0:1], 1.0 / CAP, 0.5 / CAP + 0.5, ALU.mult, ALU.add))
            link(v.tensor_scalar(prow[:, 0:1], prow[:, 0:1], MAGIC, MAGIC, ALU.add, ALU.subtract))
            v.tensor_copy(rounds[:, :], prow[:, 0:1]).then_inc(s_rounds, 1)

            dve.wait_ge(s_x, 32)
            dve.wait_ge(s_const, 6)
            with dve.Fori(0, NT) as j:
                v.bn_stats(bst[:, ds(j, 1), :].rearrange("p a d -> p (a d)"), X1[:, ds(j, 1), :].rearrange("p a d -> p (a d)")).then_inc(s_stats, 1)
            dve.wait_ge(s_stats, NT)
            norm_scale(0)
            with dve.Fori(0, NT) as j:
                v.tensor_scalar(XN[:, ds(j, 1), :].rearrange("p a d -> p (a d)"), X1[:, ds(j, 1), :].rearrange("p a d -> p (a d)"),
                                lnm[:, ds(j, 1)], lnr[:, ds(j, 1)], ALU.subtract, ALU.mult).then_inc(s_xn, 1)

            def col(n):
                return ps[:, n // 4, (n % 4) * P:(n % 4 + 1) * P]
            dve.wait_ge(s_wt, NTR)
            link(v.tensor_copy(wkvT[:, 0, :], ps[:, 0, :]))
            link(v.tensor_copy(wkvT[:, 1, :], ps[:, 1, :]))
            v.tensor_copy(woT[:, 0, :], ps[:, 2, 0:D])
            v.tensor_copy(woT[:, 1, :], ps[:, 2, D:2 * D])
            v.tensor_copy(W0T[:, 0, :], ps[:, 3, 0:P])
            v.tensor_copy(W0T[:, 1, :], ps[:, 3, P:2 * P])
            link(v.tensor_copy(W1T[:, :], ps[:, 3, 2 * P:3 * P]))
            link(v.tensor_copy(b1T[:, :, :], ps[:, 4, 0:64].rearrange("p (f e) -> p f e", e=NE)))
            link(v.tensor_copy(gvb[:, :, :], ps[:, 4, 64:64 + 2 * HD].rearrange("p (a e) -> p a e", e=HD)))
            for c in range(2):
                link(v.tensor_reduce(hm[:, c, :], wkvT[:, c, :].rearrange("p (h d) -> p h d", d=HD), AX_X, ALU.add))
                link(v.tensor_scalar(hm[:, c, :], hm[:, c, :], 1.0 / HD, None, ALU.mult))
                w = wkvT[:, c, :].rearrange("p (h d) -> p h d", d=HD)
                link(v.tensor_tensor(w, w, hm[:, c, :].unsqueeze(2).to_broadcast([P, NH, HD]), ALU.subtract))
            v.memset(zpad[:, :], 0.0).then_inc(s_wtv, 1)

            def turn(tag):
                def step(j, s):
                    dve.wait_ge(phase[tag, "turned"], j + 1)
                    ge(dve, phase[tag, "prod"], j - SLOTS + 1)
                    v.tensor_copy(work[:, s, :], ps[:, s, 0:D]).then_inc(phase[tag, "xt"], 1)
                return step

            def hsum(j, s):
                dve.wait_ge(s_sq, j + 1)
                v.tensor_reduce(hvar[:, ds(j * NH, NH)], sq[:, s, :].rearrange("p (h d) -> p h d", d=HD), AX_X, ALU.add).then_inc(s_hred, 1)
            tiles_ahead(dve, turn("mixa"), hsum)
            dve.wait_ge(s_hred, NT)
            link(v.tensor_scalar(hvar[:, :], hvar[:, :], 1.0 / HD, EPS, ALU.mult, ALU.add))
            v.engine_nop().then_inc(s_hvar, 1)
            dve.wait_ge(s_hroot, 1)
            link(v.reciprocal(hta, hrs[:, :]))
            link(v.tensor_tensor(hta, hta, hvar[:, :], ALU.mult))
            link(v.tensor_tensor(hrs[:, :], hrs[:, :], hta, ALU.add))
            link(v.tensor_scalar(hrs[:, :], hrs[:, :], 0.5, None, ALU.mult))
            link(v.reciprocal(hrs[:, :], hrs[:, :]))

            def normed(j, s):
                ge(dve, s_kvt, j - SLOTS + 1)
                v.tensor_tensor(khat[:, s, :].rearrange("p (h d) -> p h d", d=HD),
                                KC[:, ds(j, 1), :].rearrange("p a (h d) -> p (a h) d", d=HD),
                                hrs[:, ds(j * NH, NH)].unsqueeze(2).to_broadcast([P, NH, HD]), ALU.mult).then_inc(s_khat, 1)
            tiles(dve, normed)
            dve.wait_ge(s_kvt, NT)
            for c in range(2):
                sv = ps[:, 6, c * P:(c + 1) * P].rearrange("p (h d) -> p h d", d=HD)
                g_v = gvb[:, 0, :].unsqueeze(1).to_broadcast([P, 2, HD])
                b_v = gvb[:, 1, :].unsqueeze(1).to_broadcast([P, 2, HD])
                t = work[:, 0, 0:P].rearrange("p (h d) -> p h d", d=HD)
                u = work[:, 1, 0:P].rearrange("p (h d) -> p h d", d=HD)
                k2 = kvp[:, c, :].rearrange("p (h d) -> p h d", d=HD)
                link(v.tensor_tensor(k2, ps[:, 4 + c, 0:P].rearrange("p (h d) -> p h d", d=HD), g_v, ALU.mult))
                link(v.tensor_copy(kvc[:, c, 0:1], ps[:, 2 + c, 0:1]))
                link(v.tensor_scalar(t, b_v, kvc[:, c, 0:1], None, ALU.mult))
                link(v.tensor_tensor(k2, k2, t, ALU.add))
                link(v.tensor_scalar(k2, k2, cols[:, 1:2], None, ALU.mult))
                link(v.tensor_tensor(t, sv, g_v, ALU.mult))
                link(v.tensor_scalar(u, b_v, float(N), None, ALU.mult))
                link(v.tensor_tensor(t, t, u, ALU.add))
                link(v.tensor_scalar(t, t, cols[:, 2:3], None, ALU.mult))
                link(v.tensor_tensor(k2, k2, t, ALU.add))
                link(v.tensor_scalar(k2, k2, 1.0 / N, None, ALU.mult))
                link(v.memset(kvp[0:HD, c, HD:P], 0.0))
                link(v.memset(kvp[HD:P, c, 0:HD], 0.0))
            v.engine_nop().then_inc(s_kvp, 1)
            dve.wait_ge(s_t1, 1)
            v.tensor_copy(work[:, 0, :], ps[:, 0, 0:D])
            v.tensor_copy(work[:, 1, :], ps[:, 1, 0:D]).then_inc(s_t1v, 1)
            dve.wait_ge(s_m, 1)
            v.tensor_copy(M[:, 0, :], ps[:, 2, 0:D])
            v.tensor_copy(M[:, 1, :], ps[:, 3, 0:D]).then_inc(s_mv, 1)

            def mixed(j, s):
                dve.wait_ge(phase["mixb", "prod"], j + 1)
                xj = X1[:, ds(j, 1), :].rearrange("p a d -> p (a d)")
                v.tensor_tensor(xj, xj, ps[:, 5 + s % 3, 0:D], ALU.add).then_inc(phase["mixb", "read"], 1)
            tiles_ahead(dve, turn("mixb"), mixed)

            dve.wait_ge(s_recl, 16)

            def pairs(j, k, first):
                for g0, g1, _, _ in PARTS:
                    if not first:
                        dve.wait_ge(s_bmm, (j - 2) * NR + g1)
                    gw = g0 + DW
                    for g in range(g0, gw):
                        n = ds(j * NR + g, 1)
                        v.tensor_scalar(bc[k][:, g, :], iota_n[:, :], recL[:, n, 0], recL[:, n, 2], ALU.is_equal, ALU.mult)
                    for to, field, a0 in ((bc, 0, gw), (br, 1, g0)):
                        v.tensor_tensor(to[k][:, a0:g1, :], iota_n[:, :].unsqueeze(1).to_broadcast([P, g1 - a0, P]),
                                        recL[:, ds(j * NR + a0, g1 - a0), field].unsqueeze(2).to_broadcast([P, g1 - a0, P]),
                                        ALU.is_equal).then_inc(s_hot, 1)
            pairs(0, 0, True)
            pairs(1, 1, True)
            with dve.Fori(1, NT // 2) as i:
                pairs(i * 2, 0, False)
                pairs(i * 2 + 1, 1, False)
            pairs(NT - 1, 0, False)
            dve.wait_ge(s_bmm, NG)
            v.memset(HT[:, :, 8 * CHUNK:NP], 0.0).then_inc(s_tail, 1)

            dve.wait_ge(s_rounds, 1)
            with more_rounds(dve) as k:
                v.tensor_scalar(pos_all, pos_all, -float(CAP), None, ALU.add).then_inc(m_dve, 1)
                dve.wait_ge(m_dve, k * 3 - 2)
                v.tensor_scalar(big_all, pos_all, 0.0, 1.0e8, ALU.is_lt, ALU.mult).then_inc(m_dve, 1)
                v.scalar_tensor_tensor(out=low_all, in0=pos_all, scalar=float(NG), in1=key[:, 0:ET], op0=ALU.mult, op1=ALU.add).then_inc(m_dve, 1)
                dve.wait_ge(m_dve, k * 3)
                v.tensor_tensor(idx_all, low_all, big_all, ALU.add).then_inc(m_idx, 1)
                dve.wait_ge(m_recl, k * 16)
                dve.sem_inc(m_carry, 1)
                with dve.Fori(0, NT) as j:
                    tile = k * NT + j - NT
                    dve.wait_ge(m_load, tile * 16 + 16)
                    dve.sem_inc(m_carry, 1)
                    with dve.Fori(0, NR) as r:
                        block_n = tile * NR + r
                        g = ds(j * NR + r, 1)
                        v.tensor_scalar(ohc[:, 0, :], iota_n[:, :], recL[:, g, 0], recL[:, g, 2], ALU.is_equal, ALU.mult)
                        v.tensor_scalar(ohr[:, 0, :], iota_n[:, :], recL[:, g, 1], None, ALU.is_equal).then_inc(m_pair, 1)
                        dve.wait_ge(m_mm, block_n + 1)
                        part = ADJ[:, 0, :].rearrange("p (r g) -> p r g", g=NR)[:, :, ds(r, 1)].rearrange("p r a -> p (r a)")
                        v.tensor_tensor(part, part, ps[:, 7, 0:P], ALU.add).then_inc(m_add, 1)
                        dve.wait_ge(m_add, block_n + 1)

            def hrow(j, s):
                dve.wait_ge(phase["hn", "turned"], j + 1)
                v.tensor_copy(XN[:, j, :], ps[:, s, 0:D])
                v.tensor_copy(Y[:, j, :], ps[:, s, D:D + H]).then_inc(phase["hn", "read"], 1)
            for j in range(NT):
                hrow(j, j % 7)

            for l in (0, 1):
                def mx(j, s):
                    dve.wait_ge(phase[f"sm{l}", "turned"], j + 1)
                    ge(dve, s_ex[l], j - SLOTS + 1)
                    v.tensor_reduce(nmx[:, s:s + 1], ps[:, s % 3, 0:H], AX_X, ALU.max, negate=True).then_inc(s_nm[l], 1)

                def scaled(j, s):
                    dve.wait_ge(s_ex[l], j + 1)
                    v.reciprocal(rrec[:, s:s + 1], rsum[:, s:s + 1]).then_inc(s_rr[l], 1)
                    dve.wait_ge(s_rr[l], j + 1)
                    o = P01[:, ds(j, 1), l * H:(l + 1) * H].rearrange("p a d -> p (a d)")
                    if l == 0:
                        v.tensor_scalar(o, work[:, s, 0:H], rrec[:, s:s + 1], None, ALU.mult).then_inc(s_sm[0], 1)
                    else:
                        v.scalar_tensor_tensor(out=o, in0=work[:, s, 0:H], scalar=rrec[:, s:s + 1],
                                               in1=XN[:, ds(j, 1), H:2 * H].rearrange("p a d -> p (a d)"),
                                               op0=ALU.mult, op1=ALU.add).then_inc(s_sum[1], 1)
                tiles_ahead(dve, mx, scaled)
                if l == 0:
                    def summed(j, s):
                        if isinstance(j, int) and j < SLOTS:
                            dve.wait_ge(s_sm[0], NT)
                        else:
                            dve.wait_ge(s_x1h, j - SLOTS + 1)
                        v.tensor_tensor(work[:, s, 0:H], P01[:, ds(j, 1), 0:H].rearrange("p a d -> p (a d)"),
                                        XN[:, ds(j, 1), 0:H].rearrange("p a d -> p (a d)"), ALU.add).then_inc(s_sum[0], 1)

                    def added0(j, s):
                        dve.wait_ge(s_tanh[0], j + 1)
                        xj = X1[:, ds(j, 1), 0:H].rearrange("p a d -> p (a d)")
                        v.tensor_tensor(xj, xj, work[:, s, 0:H], ALU.add).then_inc(s_x1h, 1)
                    tiles_ahead(dve, summed, added0)

            def added(j, s):
                dve.wait_ge(s_tanh[1], j + 1)
                xj = X1[:, ds(j, 1), H:2 * H].rearrange("p a d -> p (a d)")
                v.tensor_tensor(xj, xj, P01[:, ds(j, 1), H:2 * H].rearrange("p a d -> p (a d)"), ALU.add).then_inc(s_x1, 1)

            def stats(j, s):
                dve.wait_ge(s_x1, j + 1)
                v.bn_stats(bst[:, ds(j, 1), :].rearrange("p a d -> p (a d)"), X1[:, ds(j, 1), :].rearrange("p a d -> p (a d)")).then_inc(s_stats, 1)
            dve.wait_ge(s_x1h, NT)
            tiles_ahead(dve, added, stats)
            dve.wait_ge(s_stats, 2 * NT)
            norm_scale(1)
            with dve.Fori(0, NT) as j:
                v.tensor_scalar(XN[:, ds(j, 1), :].rearrange("p a d -> p (a d)"), X1[:, ds(j, 1), :].rearrange("p a d -> p (a d)"),
                                lnm[:, ds(j, 1)], lnr[:, ds(j, 1)], ALU.subtract, ALU.mult).then_inc(s_xn2, 1)

            def logit(j, s):
                dve.wait_ge(phase["gate", "prod"], j + 1)
                v.tensor_copy(LG[:, ds(j, 1), :].rearrange("p a d -> p (a d)"), ps[:, 5 + s % 3, 0:NE]).then_inc(phase["gate", "read"], 1)
            tiles_ahead(dve, turn("gate"), logit)
            dve.wait_ge(phase["gate", "read"], NT)
            best, total, eid, pos, keep = (rt[:, i, :] for i in range(5))

            def wide(t):
                return t.unsqueeze(2).to_broadcast([P, NT, NE])
            iota8 = iota_n[:, 0:NE].unsqueeze(1).to_broadcast([P, NT, NE])
            link(v.tensor_reduce(best, LG[:, :, :], AX_X, ALU.max))
            link(v.tensor_tensor(tb8, LG[:, :, :], wide(best), ALU.subtract))
            v.engine_nop().then_inc(s_exp8, 1)
            link(v.tensor_scalar(tc8, tb8, 0.0, float(NE), ALU.is_lt, ALU.mult))
            link(v.tensor_tensor(tc8, tc8, iota8, ALU.add))
            link(v.tensor_reduce(eid, tc8, AX_X, ALU.min))
            link(v.tensor_tensor(OH8[:, :, :], iota8, wide(eid), ALU.is_equal))
            v.engine_nop().then_inc(s_one8, 1)
            dve.wait_ge(s_exp8, 2)
            link(v.tensor_reduce(total, ta8, AX_X, ALU.add))
            link(v.reciprocal(total, total))
            dve.wait_ge(s_cnt, 1)
            link(v.tensor_copy(tb8, ps[:, 1, 0:NT * NE].rearrange("p (t e) -> p t e", e=NE)))
            for e in range(NE):
                v.tensor_tensor_scan(out=tc8[:, :, e], data0=ones_f[:, 0:NT], data1=tb8[:, :, e], initial=0.0, op0=ALU.mult, op1=ALU.add)
            link(v.engine_nop())
            link(v.tensor_tensor(tc8, tc8, tb8, ALU.subtract))
            link(v.tensor_tensor(tc8, tc8, ps[:, 0, 0:NT * NE].rearrange("p (t e) -> p t e", e=NE), ALU.add))
            link(v.tensor_tensor(tc8, tc8, OH8[:, :, :], ALU.mult))
            link(v.tensor_reduce(pos, tc8, AX_X, ALU.add))
            link(v.tensor_scalar(keep, pos, float(CAPX), None, ALU.is_le))
            link(v.tensor_tensor(kp[:, :], keep, total, ALU.mult))
            link(v.tensor_scalar(total, pos, float(CAPX), -1.0, ALU.min, ALU.add))
            link(v.scalar_tensor_tensor(out=gidx[:, :], in0=eid, scalar=float(XS), in1=total, op0=ALU.mult, op1=ALU.add))
            link(v.tensor_scalar(keep, keep, -1.0e6, 1.0e6 - 1.0, ALU.mult, ALU.add))
            link(v.tensor_tensor(pos, pos, keep, ALU.add))
            link(v.scalar_tensor_tensor(out=sidx[:, :], in0=eid, scalar=float(XS), in1=pos, op0=ALU.mult, op1=ALU.add))
            link(v.memset(big[:, :], 10000.0))
            link(v.memset(nbig[:, :], -10000.0))
            v.engine_nop().then_inc(s_slot, 1)

            def yblock(e, s):
                for c in range(4):
                    n = min(P, CAPX - c * P)
                    dve.wait_ge(s_y, 4 * e + c + 1)
                    if c == 0:
                        ge(dve, s_yst[s], 16 * ((e - s) // 2) if isinstance(e, int) else yblock.turns)
                    v.tensor_tensor(ybs[0:n, s, c, :], ps[0:n, 5 + c % 2, 0:D], b2_b[0:n, ds(e * D, D)], ALU.add).then_inc(s_yv, 1)
            link(v.memset(ybs, 0.0))
            link(v.memset(sums[:, :], 0.0))
            dve.wait_ge(s_b2, 16)
            yblock(0, 0)
            yblock(1, 1)
            with dve.Fori(1, NE // 2) as i:
                yblock.turns = i * 16
                yblock(i * 2, 0)
                yblock(i * 2 + 1, 1)
            for j in range(NT):
                n = P if j < NT - 1 else LAST
                dve.wait_ge(s_gat[j], 16)
                v.scalar_tensor_tensor(out=XN[0:n, j, :], in0=G[0:n, j, :], scalar=kp[0:n, j:j + 1], in1=X1[0:n, j, :],
                                       op0=ALU.mult, op1=ALU.add, accum_out=sums[0:n, j:j + 1]).then_inc(s_fin, 1)
            dve.wait_ge(s_fin, NT)
            link(v.tensor_scalar(sums[:, :], sums[:, :], 0.0, None, ALU.mult))
            v.tensor_reduce(check[:, :], sums[:, :], AX_X, ALU.add).then_inc(s_check, 1)
            dve.wait_ge(s_check, 2)
            v.tensor_scalar(odd[:, :], ps[0:1, 0, 0:1], 0.0, None, ALU.not_equal).then_inc(s_odd, 1)
            dve.wait_ge(s_odd, 1)
            with dve.If(dve.value_load(odd[0:1, 0:1], min_val=0, max_val=1) > 0):
                dve.wait_ge(s_out, 16 * NT)
                for j in range(NT):
                    n = P if j < NT - 1 else LAST
                    g = G[0:n, j, :]
                    link(v.tensor_scalar(g, g, kp[0:n, j:j + 1], None, ALU.mult))
                    link(v.tensor_scalar(nanm[0:n, 0, :], g, FMAX, None, ALU.is_gt))
                    link(v.tensor_scalar(nanm[0:n, 1, :], g, -FMAX, None, ALU.is_lt))
                    link(v.copy_predicated(g, nanm[0:n, 0, :], big[0:n, :].to_broadcast([n, D])))
                    link(v.copy_predicated(g, nanm[0:n, 1, :], nbig[0:n, :].to_broadcast([n, D])))
                    link(v.tensor_tensor(nanm[0:n, 0, :], g, g, ALU.not_equal))
                    link(v.copy_predicated(g, nanm[0:n, 0, :], zpad[0:n, :].to_broadcast([n, D])))
                    v.tensor_tensor(XN[0:n, j, :], X1[0:n, j, :], g, ALU.add).then_inc(s_fixed, 1)

        @block.tensor
        def _(pe):
            pe.wait_ge(s_constv, 1)

            def ranks(t, i, par, first):
                acc = ps[0:EP, 2 * par:2 * par + 2, :].rearrange("p b n -> p (b n)")
                start = first and t < 2
                if not start:
                    pe.wait_ge(s_rankrd, t - 1)
                pe.wait_ge(s_oh, t + 1)
                for n, (lhs, s) in enumerate(((notbefore, (i - 2) % 5), (ones_b, (i - 1) % 5), (before, i % 5))):
                    for c0, c1 in ((0, 512), (512, NG)):
                        last = nc.tensor.matmul(acc[:, c0:c1], lhs[0:EP, 0:EP], oh[:, s, c0:c1],
                                                start=bool(start and n == 0), stop=True, skip_group_check=True)
                last.then_inc(s_rank, 1)
            for t in range(3 * B5):
                ranks(t, t % 5, t % 2, True)
            with pe.Fori(1, NB // 2) as m:
                for i in range(10):
                    ranks(m * 10 + 5 + i, i % 5, (1 + i) % 2, False)

            def blocks(j, par, first):
                starts = [part[0] for part in PARTS]
                weighed = 0
                for g in range(NR):
                    q, k = g // 4, g % 4
                    if g in starts:
                        c = starts.index(g)
                        pe.wait_ge(s_hot, (j * len(PARTS) + c) * 2 + 2)
                    if k == 0 and not first:
                        pe.wait_ge(s_bev, (j - 1) * 7 + q + 1)
                    if g >= starts[c] + DW:
                        weighed += 1
                        pe.wait_ge(s_wgt, j * (NR - DW * len(PARTS)) + weighed)
                    nc.tensor.matmul(ps[:, q, k * P:(k + 1) * P], bc[par][:, g, :], br[par][:, g, :], start=True, stop=True).then_inc(s_bmm, 1)
            pe.wait_ge(s_rankrd, ET)
            pe.wait_ge(s_max, 1)
            nc.tensor.transpose(ps[0:1, 7, 0:EP], pmax[:, :], ident[0:EP, 0:EP]).then_inc(s_max, 1)
            pe.wait_ge(s_w, 16 * NWL)
            def flip(dst, src, n=P):
                return nc.tensor.transpose(dst, src, ident[0:n, 0:n])
            for w, name in enumerate((wk_n, wv_n)):
                for r in range(2):
                    for c in range(2):
                        flip(ps[:, c, w * D + r * P:w * D + (r + 1) * P], name[:, r, c * P:(c + 1) * P]).then_inc(s_wt, 1)
            for r in range(2):
                for c in range(2):
                    flip(ps[:, 2, c * D + r * P:c * D + (r + 1) * P], wo_n[:, r, c * P:(c + 1) * P]).then_inc(s_wt, 1)
            for c in range(2):
                flip(ps[:, 3, c * P:(c + 1) * P], W0_n[:, c * P:(c + 1) * P]).then_inc(s_wt, 1)
            flip(ps[:, 3, 2 * P:3 * P], W1_n).then_inc(s_wt, 1)
            for f in range(8):
                flip(ps[:, 4, f * NE:(f + 1) * NE], b1_n[:, f * P:(f + 1) * P], NE).then_inc(s_wt, 1)
            nc.tensor.matmul(ps[:, 4, 64:64 + 2 * HD], ones_f[0:1, :], rows[:, 2 * D + NE:2 * D + NE + 2 * HD], start=True, stop=True).then_inc(s_wt, 1)

            def turns(tag, ready):
                def step(j, s):
                    pe.wait_ge(ready, j + 1)
                    ge(pe, phase[tag, "xt"], j - SLOTS + 1)
                    flip(ps[:, s, 0:P], XN[:, j, 0:P])
                    flip(ps[:, s, P:2 * P], XN[:, j, P:2 * P]).then_inc(phase[tag, "turned"], 1)
                return step

            def product(tag, weight, width, bias, read):
                def step(j, s):
                    pe.wait_ge(phase[tag, "xt"], j + 1)
                    ge(pe, read, j - 1)
                    o = ps[:, 5 + s % 3, 0:width]
                    nc.tensor.matmul(o, work[:, s, 0:P], weight[:, 0, :], start=True, stop=False)
                    last = nc.tensor.matmul(o, work[:, s, P:2 * P], weight[:, 1, :], start=False, stop=bias is None)
                    if bias is not None:
                        last = nc.tensor.matmul(o, ones_f[0:1, :], bias, start=False, stop=True)
                    last.then_inc(phase[tag, "prod"], 1)
                return step

            pe.wait_ge(s_wtv, 1)
            straight_ahead(turns("mixa", s_xn), product("mixa", wkvT, 2 * D, None, s_sq))

            def kvprod(j, s):
                pe.wait_ge(s_khat, j + 1)
                first = isinstance(j, int) and j == 0
                for c in range(2):
                    kh = khat[:, s, c * P:(c + 1) * P]
                    nc.tensor.matmul(ps[:, 4 + c, 0:P], kh, khat[:, s, D + c * P:D + (c + 1) * P], start=first, stop=True, skip_group_check=True)
                    nc.tensor.matmul(ps[:, 2 + c, 0:1], kh, ones_f[:, 0:1], start=first, stop=True, skip_group_check=True)
                nc.tensor.matmul(ps[:, 6, 0:D], ones_f[:, :], khat[:, s, D:2 * D], start=first, stop=True, skip_group_check=True).then_inc(s_kvt, 1)
            tiles(pe, kvprod)
            pe.wait_ge(s_kvp, 1)
            for c in range(2):
                last = nc.tensor.matmul(ps[:, c, 0:D], kvp[:, c, :], wq_n[:, c, :], start=True, stop=True)
            last.then_inc(s_t1, 1)
            pe.wait_ge(s_t1v, 1)
            for i in range(2):
                for c in range(2):
                    last = nc.tensor.matmul(ps[:, 2 + i, 0:D], work[:, c, i * P:(i + 1) * P], woT[:, c, :], start=(c == 0), stop=(c == 1))
            last.then_inc(s_m, 1)
            pe.wait_ge(s_mv, 1)
            straight_ahead(turns("mixb", s_xn), product("mixb", M, D, bo_r, phase["mixb", "read"]))
            pe.wait_ge(phase["mixb", "read"], NT)

            blocks(0, 0, True)
            blocks(1, 1, False)
            with pe.Fori(1, NT // 2) as i:
                blocks(i * 2, 0, False)
                blocks(i * 2 + 1, 1, False)
            blocks(NT - 1, 0, False)

            pe.wait_ge(s_bev, 7 * NT)
            with more_rounds(pe) as k:
                with pe.Fori(0, NG) as g:
                    block_n = k * NG + g - NG
                    pe.wait_ge(m_pair, block_n + 1)
                    nc.tensor.matmul(ps[:, 7, 0:P], ohc[:, 0, :], ohr[:, 0, :], start=True, stop=True).then_inc(m_mm, 1)
                    pe.wait_ge(m_add, block_n + 1)

            def spmm1(half):
                def tile(j, slot, loaded, first):
                    pe.wait_ge(s_ald[slot], loaded)
                    pe.wait_ge(s_stage, half * NT + j + 1)
                    for dd in range(2):
                        for q in range(4):
                            last = nc.tensor.matmul(ps[:, dd * 4 + q, 0:CHUNK], stage[:, slot, dd * H:(dd + 1) * H],
                                                    ADJ[:, slot, q * CHUNK:(q + 1) * CHUNK], start=first, stop=True, skip_group_check=True)
                    last.then_inc(s_tile, 1)
                if half == 0:
                    pe.wait_ge(s_bev, 7 * NT)
                else:
                    pe.wait_ge(s_acc, 8)
                r = NT // SLOTS
                for j in range(SLOTS):
                    tile(j, j, (half * r + 1) * 16, j == 0)
                with pe.Fori(1, r) as i:
                    for j in range(SLOTS):
                        tile(i * SLOTS + j, j, (i + half * r + 1) * 16, False)
            spmm1(0)
            spmm1(1)

            pe.wait_ge(s_acc, 16)
            pe.wait_ge(s_tail, 1)
            for j in range(NT):
                b = j % 7
                ge(pe, phase["hn", "read"], j - 6)
                t = [HT[:, c, j * P:(j + 1) * P] for c in range(2)]
                flip(ps[:, b, 0:P], t[0])
                flip(ps[:, b, P:2 * P], t[1])
                nc.tensor.matmul(ps[:, b, D:D + H], t[0], W0T[:, 0, :], start=True, stop=False, skip_group_check=True)
                nc.tensor.matmul(ps[:, b, D:D + H], t[1], W0T[:, 1, :], start=False, stop=True, skip_group_check=True).then_inc(phase["hn", "turned"], 1)
            pe.wait_ge(phase["hn", "read"], NT)

            for l in (0, 1):
                def ztile(j, s):
                    k = (2 + l) * (NT // SLOTS)
                    pe.wait_ge(s_ald[s], (k + 1) * 16 if isinstance(j, int) else (ztile.i + k + 1) * 16)
                    pe.wait_ge(s_stage, (2 + l) * NT + j + 1)
                    first = isinstance(j, int) and j == 0
                    for q in range(8):
                        last = nc.tensor.matmul(ps[:, q, 0:CHUNK], stage[:, s, 0:H], ADJ[:, s, q * CHUNK:(q + 1) * CHUNK],
                                                start=first, stop=True, skip_group_check=True)
                    last.then_inc(s_zt[l], 1)
                for j in range(SLOTS):
                    ztile(j, j)
                with pe.Fori(1, NT // SLOTS) as i:
                    ztile.i = i
                    for s in range(SLOTS):
                        ztile(i * SLOTS + s, s)

                for j in range(NT):
                    pe.wait_ge(s_z[l], min(max(3, (j * P + P - 1) // CHUNK + 1), 8))
                    ge(pe, s_ex[l], j - 1)
                    o = ps[:, j % SLOTS % 3, 0:H]
                    t = HT[:, 0, j * P:(j + 1) * P]
                    if l == 0:
                        flip(o, t).then_inc(phase["sm0", "turned"], 1)
                    else:
                        nc.tensor.matmul(o, t, W1T[:, :], start=True, stop=False)
                        nc.tensor.matmul(o, ones_f[0:1, :], gb1_r, start=False, stop=True).then_inc(phase["sm1", "turned"], 1)
                pe.wait_ge(s_ex[l], NT)

            straight_ahead(turns("gate", s_xn2), product("gate", gate_w, NE, gate_b, phase["gate", "read"]))
            pe.wait_ge(s_one8, 1)
            oh8 = OH8[:, :, :].rearrange("p t e -> p (t e)")
            nc.tensor.matmul(ps[:, 0, 0:NT * NE], upto[:, :], oh8, start=True, stop=True)
            nc.tensor.matmul(ps[:, 1, 0:NT * NE], ones_f[:, :], oh8, start=True, stop=True).then_inc(s_cnt, 1)

            pe.wait_ge(s_slot, 1)

            def rows_in(e, s, loaded):
                pe.wait_ge(s_wl[s], loaded)
                ge(pe, s_xbv, 2 * e)
                for c in range(2):
                    for b in range(4):
                        last = flip(ps[:, c, b * P:(b + 1) * P], xbs[:, s, b, c * P:(c + 1) * P])
                    last.then_inc(s_xbt, 1)

            def up(e, s):
                pe.wait_ge(s_xbv, 2 * e + 2)
                for f in range(8):
                    ge(pe, s_hidv, 8 * e + f - 2)
                    for c in range(2):
                        last = nc.tensor.matmul(ps[:, 2 + f % 3, 0:CAPX], w1s[:, s, c, f * P:(f + 1) * P], xbT[:, s, c, 0:CAPX],
                                                start=(c == 0), stop=(c == 1))
                    last.then_inc(s_hid, 1)

            def down(e, s):
                pe.wait_ge(s_hidv, 8 * e + 8)
                for c in range(4):
                    n = min(P, CAPX - c * P)
                    ge(pe, s_yv, 4 * e + c - 1)
                    o = ps[0:n, 5 + c % 2, 0:D]
                    for f in range(8):
                        last = nc.tensor.matmul(o, hmT[:, f, c * P:c * P + n], w2s[:, s, f, :], start=(f == 0), stop=(f == 7))
                    last.then_inc(s_y, 1)
            rows_in(0, 0, 48)
            up(0, 0)
            rows_in(1, 1, 48)
            down(0, 0)
            with pe.Fori(1, NE // 2) as i:
                up(i * 2 - 1, 1)
                rows_in(i * 2, 0, (i + 1) * 48)
                down(i * 2 - 1, 1)
                up(i * 2, 0)
                rows_in(i * 2 + 1, 1, (i + 1) * 48)
                down(i * 2, 0)
            up(NE - 1, 1)
            down(NE - 1, 1)
            pe.wait_ge(s_check, 1)
            nc.tensor.matmul(ps[0:1, 0, 0:1], check[:, :], ones_f[:, 0:1], start=True, stop=True).then_inc(s_check, 1)


_INS = ["x", "src", "dst", "edge_weight", "L0_gnn_W0", "L0_gnn_b0", "L0_gnn_W1", "L0_gnn_b1", "L0_mix_wq", "L0_mix_wk", "L0_mix_wv",
        "L0_mix_wo", "L0_mix_bo", "L0_mix_ln_k_g", "L0_mix_ln_k_b", "L0_mix_ln_v_g", "L0_mix_ln_v_b", "L0_ffn_gate_w", "L0_ffn_gate_b",
        "L0_ffn_w1", "L0_ffn_b1", "L0_ffn_w2", "L0_ffn_b2"]


def kernel(**inputs):
    import numpy as np
    import concourse.bacc as bacc
    from concourse.bass_utils import run_bass_kernel_spmd

    nc = bacc.Bacc("TRN2", target_bir_lowering=False, num_devices=1)
    arrays, aps = {}, {}
    for name in _INS:
        v = np.ascontiguousarray(inputs[name])
        arrays[f"in_{name}"] = v
        aps[name] = nc.dram_tensor(f"in_{name}", v.shape, mybir.dt.from_np(v.dtype), kind="ExternalInput").ap()
    out = nc.dram_tensor("out_0", (N, D), F32, kind="ExternalOutput").ap()
    graph_program(nc, aps, out)
    r = run_bass_kernel_spmd(nc, [arrays], core_ids=[0])
    return r.results[0]["out_0"]
```

```python
from contextlib import ExitStack, contextmanager

import concourse.bass as bass
from concourse import mybir
from concourse.alu_op_type import AluOpType as ALU

F32 = mybir.dt.float32
BF16 = mybir.dt.bfloat16
F16 = mybir.dt.float16
I32 = mybir.dt.int32
ACT = mybir.ActivationFunctionType
AX_X = mybir.AxisListType.X
ds = bass.ds

N = 3125
E = 53125
D = 256
H = 128
P = 128
NT = 25
NE = 8
CAPX = 489
XS = 512
F = 1024
NH = 8
HD = 64
FMAX = 3.4028234663852886e38
LAST = N - (NT - 1) * P
NP = NT * P
NR = 25
NG = NT * NR
CAP = P
EP = 125
ET = E // EP
B5 = 5
NB = ET // B5
AHEAD = 3
STATS_M = 1 + (NT - 1) // 3
MIX_M = NB // 2 - NT
MAGIC = float(1.5 * 2 ** 23)
CHUNK = 391
EPS = 1e-5
NWL = 18
NTR = 23
PARTS = ((0, 8, 0, 2), (8, 16, 2, 4), (16, NR, 4, 7))
DW = 3
SLOTS = 5


def ge(eng, semaphore, value):
    if not isinstance(value, int) or value > 0:
        eng.wait_ge(semaphore, value)


def tiles(eng, step):
    for j in range(SLOTS):
        step(j, j)
    with eng.Fori(1, NT // SLOTS) as i:
        for s in range(SLOTS):
            step(i * SLOTS + s, s)


def tiles_ahead(eng, ahead, step):
    ahead(0, 0)
    for j in range(SLOTS):
        ahead(j + 1, (j + 1) % SLOTS)
        step(j, j)
    with eng.Fori(1, NT // SLOTS - 1) as i:
        for s in range(SLOTS):
            ahead(i * SLOTS + s + 1, (s + 1) % SLOTS)
            step(i * SLOTS + s, s)
    for s in range(SLOTS):
        j = NT - SLOTS + s
        if j + 1 < NT:
            ahead(j + 1, (s + 1) % SLOTS)
        step(j, s)


def graph_program(nc, a, out):
    ctx = ExitStack()
    with ctx:
        def sb(name, shape, dt=F32):
            return ctx.enter_context(nc.sbuf_tensor(name, shape, dt))

        def sem(name):
            return ctx.enter_context(nc.semaphore(name))

        def dram(name, shape, dt=F32):
            return nc.dram_tensor(name, shape, dt, kind="Internal").ap()

        rec_dram = dram("rec_dram", [CAP * NG, 4])
        adj_dram = dram("adj_dram", [NT, P, NP])

        xbuf_dram = dram("xbuf_dram", [NE * XS, D])
        ybuf_dram = dram("ybuf_dram", [NE * XS, D])

        X1 = sb("X1", [P, NT, D])
        XN = sb("XN", [P, NT, D])
        HT = sb("HT", [P, 2, NP])
        ADJ = sb("ADJ", [P, SLOTS, NP])
        P01 = sb("P01", [P, NT, D])
        Y = sb("Y", [P, NT, H])
        stage = sb("stage", [P, SLOTS, D])
        p01 = P01[:, :, :].rearrange("p t d -> p (t d)")
        src_i = p01[0:EP, 0:ET].bitcast(I32)
        dst_i = p01[0:EP, ET:2 * ET].bitcast(I32)
        val = p01[0:EP, 2 * ET:3 * ET]
        srcf = p01[0:EP, 3 * ET:4 * ET]
        dstf = p01[0:EP, 4 * ET:5 * ET]
        quo = p01[0:EP, 5 * ET:6 * ET]
        key = p01[0:EP, 6 * ET:6 * ET + ET + AHEAD]
        pos_all = p01[0:EP, 7 * ET + AHEAD:8 * ET + AHEAD]
        rec = p01[0:EP, 8 * ET + AHEAD:12 * ET + AHEAD].rearrange("p (t f) -> p t f", f=4)
        yf = Y[:, :, :].rearrange("p t d -> p (t d)")
        recL = yf[:, 0:NG * 4].rearrange("p (g f) -> p g f", f=4)
        adjf = ADJ[:, :, :].rearrange("p s n -> p (s n)")
        zeros = adjf[:, 3200:3200 + NG * 4]
        iota_i = adjf[:, 6400:6400 + 640].bitcast(I32)
        iota_g = sb("iota_g", [P, 640], F16)
        iota_n = sb("iota_n", [P, P])
        ones_f = sb("ones_f", [P, P])
        ident = sb("ident", [P, P])
        before_f = sb("before_f", [P, P])
        before = sb("before", [P, P], BF16)
        upto = sb("upto", [P, P])
        notbefore = sb("notbefore", [P, P], BF16)
        ones_b = sb("ones_b", [P, P], BF16)
        pos5 = sb("pos5", [EP, 2, B5])
        idx5 = sb("idx5", [EP, 2, B5], I32)
        rec5 = sb("rec5", [EP, 2, B5, 4])
        carrier = sb("carrier", [P, 4])
        work = sb("work", [P, SLOTS, D])
        ohc = work[:, :, 0:P]
        ohr = work[:, :, P:2 * P]
        idx_all = dst_i
        big_all = srcf
        low_all = dstf
        pmax = sb("pmax", [EP, 1])
        prow = sb("prow", [1, P])
        rounds = sb("rounds", [1, 1], I32)
        htf = HT[:, :, :].rearrange("p c n -> p (c n)")
        ohf = htf[0:EP, 3968:5568]
        oh = ohf.bitcast(BF16).rearrange("p (s n) -> p s n", s=5)
        junk = htf[0:EP, 5568:6208].bitcast(BF16).rearrange("p (s n) -> p s n", s=2)
        wk_n = htf[:, 0:512].rearrange("p (r n) -> p r n", r=2)
        wv_n = htf[:, 512:1024].rearrange("p (r n) -> p r n", r=2)
        wo_n = htf[:, 1024:1536].rearrange("p (r n) -> p r n", r=2)
        W0_n = htf[:, 1536:1792]
        W1_n = htf[:, 1792:1920]
        b1_n = htf[0:NE, 1920:2944]
        wkvT = htf[:, 2944:3968].rearrange("p (c n) -> p c n", c=2)
        wq_n = p01[:, 5104:5616].rearrange("p (r n) -> p r n", r=2)
        woT = p01[:, 5616:6128].rearrange("p (r n) -> p r n", r=2)
        W0T = sb("W0T", [P, 2, H])
        W1T = sb("W1T", [P, H])
        b1T = sb("b1T", [P, F // P, NE])
        gate_w = sb("gate_w", [P, 2, NE])
        rows = sb("rows", [1, 2 * D + NE + 2 * D])
        bo_r = rows[:, 0:D]
        gb1_r = rows[:, D:D + H]
        gate_b = rows[:, D + H:D + H + NE]
        vg_r = rows[:, 2 * D + NE:2 * D + NE + HD]
        vb_r = rows[:, 2 * D + NE + HD:2 * D + NE + 2 * HD]
        cols = sb("cols", [P, 4])
        gvb = sb("gvb", [P, 2, HD])
        hm = sb("hm", [P, 2, NH])
        KC = adjf[:, 0:NT * 512].rearrange("p (t n) -> p t n", t=NT)
        sq = adjf[:, NT * 512:NT * 512 + SLOTS * 512].rearrange("p (s n) -> p s n", s=SLOTS)
        hvar = sb("hvar", [P, NT * NH])
        hrs = sb("hrs", [P, NT * NH])
        hta = adjf[:, NT * 512 + SLOTS * 512:NT * 512 + SLOTS * 512 + NT * NH]
        khat = sq
        kvp = sb("kvp", [P, 2, P])
        kvc = sb("kvc", [P, 2, 4])
        M = sb("M", [P, 2, D])
        bc = [HT[:, k, :].rearrange("p (g n) -> p g n", g=NR) for k in range(2)]
        br = [ADJ[:, 2 + k, :].rearrange("p (g n) -> p g n", g=NR) for k in range(2)]
        nmx = sb("nmx", [P, SLOTS])
        rsum = sb("rsum", [P, SLOTS])
        rrec = sb("rrec", [P, SLOTS])
        LT = p01[0:NE, 0:NP]
        LG = yf[:, 0:NT * NE].rearrange("p (t e) -> p t e", e=NE)
        OH8 = yf[:, NT * NE:2 * NT * NE].rearrange("p (t e) -> p t e", e=NE)
        ta8 = kvp[:, :, :].rearrange("p a b -> p (a b)")[:, 0:NT * NE].rearrange("p (t e) -> p t e", e=NE)
        tb8 = M[:, 0, 0:NT * NE].rearrange("p (t e) -> p t e", e=NE)
        tc8 = M[:, 1, 0:NT * NE].rearrange("p (t e) -> p t e", e=NE)
        rt = yf[:, 2 * NT * NE:3 * NT * NE].rearrange("p (a t) -> p a t", t=NT)
        sidx = sb("sidx", [P, NT], I32)
        gidx = sb("gidx", [P, NT], I32)
        kp = sb("kp", [P, NT])
        w1s = adjf[:, 0:4096].rearrange("p (s c f) -> p s c f", s=2, c=2)
        w2s = adjf[:, 4096:8192].rearrange("p (s c f) -> p s c f", s=2, c=8)
        xbs = adjf[:, 8192:10240].rearrange("p (s c f) -> p s c f", s=2, c=4)
        xbT = adjf[:, 10240:12288].rearrange("p (s c f) -> p s c f", s=2, c=2)
        b2_b = adjf[:, 12288:12288 + NE * D]
        hmT = htf[:, 0:4096].rearrange("p (c f) -> p c f", c=8)
        ybs = htf[:, 4096:6144].rearrange("p (s c f) -> p s c f", s=2, c=4)
        G = P01
        big = sb("big", [P, 1])
        nbig = sb("nbig", [P, 1])
        zpad = sb("zpad", [P, 1])
        sums = sb("sums", [P, NT])
        check = sb("check", [P, 1])
        odd = sb("odd", [1, 1], I32)
        nanm = work[:, 0:2, :].bitcast(I32)
        bst = sb("bst", [P, NT, 6])
        lnm = sb("lnm", [P, NT])
        lnr = sb("lnr", [P, NT])
        lna = sb("lna", [P, NT])
        lnb = sb("lnb", [P, NT])

        ps = ctx.enter_context(nc.psum_tensor("ps", [P, 8, 512], F32))

        s_edge = sem("s_edge")
        s_x = sem("s_x")
        s_zero = sem("s_zero")
        s_recz = sem("s_recz")
        s_const = sem("s_const")
        s_constv = sem("s_constv")
        s_dve = sem("s_dve")
        s_oh = sem("s_oh")
        s_rank = sem("s_rank")
        s_rankrd = sem("s_rankrd")
        s_idx = sem("s_idx")
        s_rec = sem("s_rec")
        s_prep = sem("s_prep")
        s_scat = [sem(f"s_scat{i}") for i in range(2)]
        s_recl = sem("s_recl")
        s_hot = sem("s_hot")
        s_wgt = sem("s_wgt")
        s_tail = sem("s_tail")
        s_bmm = sem("s_bmm")
        s_bev = sem("s_bev")
        s_ast = [sem(f"s_ast{i}") for i in range(2)]
        s_ald = [sem(f"s_ald{i}") for i in range(SLOTS)]
        s_stage = sem("s_stage")
        s_xn = sem("s_xn")
        s_stats = sem("s_stats")
        s_var = sem("s_var")
        s_root = sem("s_root")
        s_carry = sem("s_carry")
        s_tile = sem("s_tile")
        s_acc = sem("s_acc")
        s_w = sem("s_w")
        s_wt = sem("s_wt")
        s_wtc = sem("s_wtc")
        s_wtv = sem("s_wtv")
        s_gv = sem("s_gv")
        s_xz = sem("s_xz")
        phase = {}
        for tag, steps in (("mixa", "staged turned xt prod"), ("mixb", "staged turned xt prod read"), ("gate", "turned xt prod read back"),
                           ("hn", "turned read"), ("sm0", "turned"), ("sm1", "turned")):
            for what in steps.split():
                phase[tag, what] = sem(f"{tag}_{what}")
        s_sq = sem("s_sq")
        s_hvar = sem("s_hvar")
        s_hroot = sem("s_hroot")
        s_khat = sem("s_khat")
        s_kvt = sem("s_kvt")
        s_kvp = sem("s_kvp")
        s_t1 = sem("s_t1")
        s_t1v = sem("s_t1v")
        s_m = sem("s_m")
        s_mv = sem("s_mv")
        s_z = {l: sem(f"s_z{l}") for l in (0, 1)}
        s_zt = {l: sem(f"s_zt{l}") for l in (0, 1)}
        s_nm = {l: sem(f"s_nm{l}") for l in (0, 1)}
        s_ex = {l: sem(f"s_ex{l}") for l in (0, 1)}
        s_rr = {l: sem(f"s_rr{l}") for l in (0, 1)}
        s_sm = {l: sem(f"s_sm{l}") for l in (0, 1)}
        s_sum = [sem(f"s_sum{l}") for l in (0, 1)]
        s_tanh = [sem(f"s_tanh{l}") for l in (0, 1)]
        s_x1h = sem("s_x1h")
        s_x1 = sem("s_x1")
        s_xn2 = sem("s_xn2")
        s_exp8 = sem("s_exp8")
        s_one8 = sem("s_one8")
        s_cnt = sem("s_cnt")
        s_slot = sem("s_slot")
        s_disp = sem("s_disp")
        s_b2 = sem("s_b2")
        s_wl = [sem(f"s_wl{i}") for i in range(2)]
        s_xbt = sem("s_xbt")
        s_xbv = sem("s_xbv")
        s_hid = sem("s_hid")
        s_hidv = sem("s_hidv")
        s_y = sem("s_y")
        s_yv = sem("s_yv")
        s_yst = [sem(f"s_yst{i}") for i in range(2)]
        s_gat = [sem(f"s_gat{j}") for j in range(NT)]
        s_max = sem("s_max")
        s_rounds = sem("s_rounds")
        m_dve = sem("m_dve")
        m_carry = sem("m_carry")
        m_own = sem("m_own")
        m_copy = sem("m_copy")
        m_idx = sem("m_idx")
        m_zero = sem("m_zero")
        m_clear = sem("m_clear")
        m_scat = sem("m_scat")
        m_recl = sem("m_recl")
        m_load = sem("m_load")
        m_store = sem("m_store")
        m_pair = sem("m_pair")
        m_mm = sem("m_mm")
        m_add = sem("m_add")
        s_fin = sem("s_fin")
        s_check = sem("s_check")
        s_odd = sem("s_odd")
        s_fixed = sem("s_fixed")
        s_again = sem("s_again")
        s_out = sem("s_out")

        @contextmanager
        def more_rounds(eng):
            count = eng.value_load(rounds[0:1, 0:1], min_val=1, max_val=E // CAP + 1)
            with eng.If(count > 1):
                with eng.Fori(1, count) as k:
                    yield k

        block = ctx.enter_context(nc.Block())

        @block.sync
        def _(sp):
            sp.dma_start(src_i, a["src"].rearrange("(p t) -> p t", t=ET)).then_inc(s_edge, 16)
            sp.dma_start(dst_i, a["dst"].rearrange("(p t) -> p t", t=ET)).then_inc(s_edge, 16)
            sp.dma_start(val, a["edge_weight"].rearrange("(p t) -> p t", t=ET)).then_inc(s_edge, 16)
            row = lambda name: a[name].rearrange("(a n) -> a n", a=1)
            half = lambda name: a[name].rearrange("(r p) n -> p r n", p=P)
            for dst, src in ((wk_n, half("L0_mix_wk")), (wv_n, half("L0_mix_wv")), (wo_n, half("L0_mix_wo")), (wq_n[:, :, :], half("L0_mix_wq")),
                             (W0_n, a["L0_gnn_W0"]), (W1_n, a["L0_gnn_W1"]), (b1_n, a["L0_ffn_b1"]), (gate_w[:, :, :], half("L0_ffn_gate_w")),
                             (bo_r, row("L0_mix_bo")), (gb1_r, row("L0_gnn_b1")), (gate_b, row("L0_ffn_gate_b")),
                             (vg_r, row("L0_mix_ln_v_g")), (vb_r, row("L0_mix_ln_v_b")),
                             (cols[:, 0:1], a["L0_gnn_b0"].rearrange("(p a) -> p a", a=1)),
                             (cols[0:HD, 1:2], a["L0_mix_ln_k_g"].rearrange("(p a) -> p a", a=1)),
                             (cols[HD:P, 1:2], a["L0_mix_ln_k_g"].rearrange("(p a) -> p a", a=1)),
                             (cols[0:HD, 2:3], a["L0_mix_ln_k_b"].rearrange("(p a) -> p a", a=1)),
                             (cols[HD:P, 2:3], a["L0_mix_ln_k_b"].rearrange("(p a) -> p a", a=1))):
                sp.dma_start(dst, src).then_inc(s_w, 16)
            sp.wait_ge(s_zero, 3)
            sp.dma_start(rec_dram.rearrange("(s g) f -> s (g f)", g=NG), zeros).then_inc(s_recz, 16)
            sp.dma_start(X1[:, 0:NT - 1, :], a["x"][0:(NT - 1) * P, :].rearrange("(j p) d -> p j d", p=P)).then_inc(s_x, 16)
            sp.wait_ge(s_const, 6)
            sp.dma_start(X1[0:LAST, NT - 1, :], a["x"][(NT - 1) * P:N, :]).then_inc(s_x, 16)
            for i in range(4):
                sp.dma_start(xbuf_dram.rearrange("(p c) d -> p (c d)", p=P)[:, i * 2048:(i + 1) * 2048], zeros[:, 0:2048]).then_inc(s_xz, 16)
            sp.wait_ge(s_scat[0], 16 * B5 * ((NB + 1) // 2))
            sp.wait_ge(s_scat[1], 16 * B5 * (NB // 2))
            sp.dma_start(recL.rearrange("p g f -> p (g f)"), rec_dram.rearrange("(s g) f -> s (g f)", g=NG)).then_inc(s_recl, 16)
            def store(j, slot):
                sp.wait_ge(s_bev, 7 * (j + 1))
                sp.dma_start(adj_dram[ds(j, 1), :, :].rearrange("a p n -> p (a n)"), ADJ[:, slot, :]).then_inc(s_ast[slot], 16)
            with sp.Fori(0, NT // 2) as i:
                store(i * 2, 0)
                store(i * 2 + 1, 1)
            store(NT - 1, 0)
            sp.wait_ge(s_ast[0], 16 * (NT // 2 + 1))
            sp.wait_ge(s_ast[1], 16 * (NT // 2))
            sp.wait_ge(s_rounds, 1)
            with more_rounds(sp) as k:
                sp.wait_ge(m_zero, k)
                sp.dma_start(rec_dram.rearrange("(s g) f -> s (g f)", g=NG), zeros).then_inc(m_clear, 16)
                sp.wait_ge(m_scat, 16 * ET)
                sp.dma_start(recL.rearrange("p g f -> p (g f)"), rec_dram.rearrange("(s g) f -> s (g f)", g=NG)).then_inc(m_recl, 16)
                with sp.Fori(0, NT) as j:
                    tile = k * NT + j - NT
                    sp.dma_start(ADJ[:, 0, :], adj_dram[ds(j, 1), :, :].rearrange("a p n -> p (a n)")).then_inc(m_load, 16)
                    sp.wait_ge(m_add, tile * NR + NR)
                    sp.dma_start(adj_dram[ds(j, 1), :, :].rearrange("a p n -> p (a n)"), ADJ[:, 0, :]).then_inc(m_store, 16)
                    sp.wait_ge(m_store, tile * 16 + 16)
                    sp.sem_inc(m_carry, 1)
            for half in range(2):
                def load(j, slot, first):
                    if not (first and half == 0):
                        sp.wait_ge(s_tile, half * NT + j - SLOTS + 1)
                    sp.dma_start(ADJ[:, slot, 0:4 * CHUNK],
                                 adj_dram[ds(j, 1), :, half * 4 * CHUNK:(half + 1) * 4 * CHUNK].rearrange("a p n -> p (a n)")).then_inc(s_ald[slot], 16)
                for j in range(SLOTS):
                    load(j, j, True)
                with sp.Fori(1, NT // SLOTS) as i:
                    for j in range(SLOTS):
                        load(i * SLOTS + j, j, False)
            for l in (0, 1):
                def load(j, slot):
                    if l == 0:
                        if isinstance(j, int):
                            sp.wait_ge(s_tile, 2 * NT - SLOTS + 1 + j)
                        else:
                            sp.wait_ge(s_zt[0], j - SLOTS + 1)
                    else:
                        if isinstance(j, int):
                            sp.wait_ge(s_zt[0], NT - SLOTS + 1 + j)
                        else:
                            sp.wait_ge(s_zt[1], j - SLOTS + 1)
                    sp.dma_start(ADJ[:, slot, 0:8 * CHUNK], adj_dram[ds(j, 1), :, 0:8 * CHUNK].rearrange("a p n -> p (a n)")).then_inc(s_ald[slot], 16)
                tiles(sp, load)
            sp.wait_ge(s_zt[1], NT)
            sp.dma_start(b2_b, a["L0_ffn_b2"].rearrange("e d -> (e d)").partition_broadcast(P)).then_inc(s_b2, 16)

            def weights(e, s):
                sp.dma_start(w1s[:, s, :, :], a["L0_ffn_w1"][ds(e, 1), :, :].rearrange("a (c p) f -> p (a c) f", p=P)).then_inc(s_wl[s], 16)
                sp.dma_start(w2s[:, s, :, :], a["L0_ffn_w2"][ds(e, 1), :, :].rearrange("a (c p) f -> p (a c) f", p=P)).then_inc(s_wl[s], 16)

            def tokens(e, s):
                sp.dma_start(xbs[:, s, :, :], xbuf_dram[ds(e * XS, XS), :].rearrange("(c p) f -> p c f", p=P)).then_inc(s_wl[s], 16)

            def ystore(e, s):
                sp.wait_ge(s_yv, 4 * (e + 1))
                sp.dma_start(ybuf_dram[ds(e * XS, XS), :].rearrange("(c p) f -> p c f", p=P), ybs[:, s, :, :]).then_inc(s_yst[s], 16)
            weights(0, 0)
            weights(1, 1)
            sp.wait_ge(s_disp, 16 * NT)
            tokens(0, 0)
            tokens(1, 1)
            with sp.Fori(0, NE // 2 - 1) as i:
                for s in range(2):
                    ystore(i * 2 + s, s)
                    weights(i * 2 + s + 2, s)
                    tokens(i * 2 + s + 2, s)
            for s in range(2):
                ystore(NE - 2 + s, s)
            for j in range(NT):
                sp.wait_ge(s_fin, j + 1)
                n = P if j < NT - 1 else LAST
                sp.dma_start(out[j * P:j * P + n, :], XN[0:n, j, :]).then_inc(s_out, 16)
            sp.wait_ge(s_odd, 1)
            with sp.If(sp.value_load(odd[0:1, 0:1], min_val=0, max_val=1) > 0):
                for j in range(NT):
                    n = P if j < NT - 1 else LAST
                    sp.wait_ge(s_fixed, j + 1)
                    sp.dma_start(out[j * P:j * P + n, :], XN[0:n, j, :]).then_inc(s_again, 16)
                sp.wait_ge(s_again, 16 * NT)
            sp.wait_ge(s_out, 16 * NT)

        @block.gpsimd
        def _(gp):
            gp.memset(zeros, 0.0).then_inc(s_zero, 1)
            gp.memset(ohf, 0.0).then_inc(s_zero, 1)
            gp.memset(carrier[:, :], 0.0).then_inc(s_zero, 1)
            gp.iota(iota_i, pattern=[[1, 640]], base=0, channel_multiplier=0).then_inc(s_const, 1)
            gp.memset(ones_f[:, :], 1.0).then_inc(s_const, 1)
            gp.wait_ge(s_const, 2)
            gp.affine_select(out=before_f[:, :], in_=ones_f[:, :], compare_op=ALU.is_gt, fill=0.0,
                             base=0, pattern=[[1, P]], channel_multiplier=-1).then_inc(s_const, 1)
            gp.affine_select(out=ident[:, :], in_=ones_f[:, :], compare_op=ALU.is_equal, fill=0.0,
                             base=0, pattern=[[1, P]], channel_multiplier=-1).then_inc(s_const, 1)
            gp.affine_select(out=upto[:, :], in_=ones_f[:, :], compare_op=ALU.is_ge, fill=0.0,
                             base=0, pattern=[[1, P]], channel_multiplier=-1).then_inc(s_const, 1)
            gp.memset(X1[:, NT - 1, :], 0.0).then_inc(s_const, 1)
            gp.wait_ge(s_recz, 16)
            gp.wait_ge(s_zero, 3)

            def scatter(b, q):
                gp.wait_ge(s_idx, b + 1)
                gp.wait_ge(s_rec, b + 1)
                if not isinstance(b, int):
                    gp.wait_ge(s_carry, b)
                gp.tensor_tensor(carrier[:, 0:1], carrier[:, 1:2], carrier[:, 2:3], ALU.add).then_inc(s_carry, 1)
                for i in range(B5):
                    gp.indirect_dma_start(rec_dram[:, :], bass.IndirectOffsetOnAxis(ap=idx5[:, q, i:i + 1], axis=0),
                                          rec5[:, q, i, :], None, bounds_check=CAP * NG - 1, oob_is_err=False).then_inc(s_scat[q], 16)
            scatter(0, 0)
            with gp.Fori(0, NB // 2) as m:
                scatter(m * 2 + 1, 1)
                scatter(m * 2 + 2, 0)

            gp.wait_ge(s_xn, NT)
            gp.wait_ge(phase["mixa", "turned"], NT)

            def staged(j, first):
                if not first:
                    gp.wait_ge(phase["mixb", "turned"], j)
                    gp.tensor_tensor(carrier[:, 0:1], carrier[:, 1:2], carrier[:, 2:3], ALU.add).then_inc(s_carry, 1)
                gp.tensor_copy(stage[:, 0, :], XN[:, ds(j, 1), :].rearrange("p a d -> p (a d)")).then_inc(phase["mixb", "staged"], 1)
                gp.wait_ge(s_carry, j + NB)
            staged(0, True)
            with gp.Fori(1, NT) as j:
                staged(j, False)

            gp.wait_ge(s_ast[0], 16 * (NT // 2 + 1))
            gp.wait_ge(s_ast[1], 16 * (NT // 2))
            gp.wait_ge(s_rounds, 1)
            with more_rounds(gp) as k:
                gp.wait_ge(m_idx, k)
                gp.sem_inc(m_carry, 1)
                gp.memset(zeros, 0.0).then_inc(m_zero, 1)
                gp.wait_ge(m_clear, k * 16)
                gp.sem_inc(m_carry, 1)
                with gp.Fori(0, NB) as b:
                    batch = k * NB + b - NB
                    gp.tensor_copy(idx5[:, 0, :], idx_all[:, ds(b * B5, B5)]).then_inc(m_copy, 1)
                    gp.tensor_copy(rec5[:, 0, :, :], rec[:, ds(b * B5, B5), :]).then_inc(m_copy, 1)
                    gp.wait_ge(m_copy, batch * 2 + 2)
                    gp.tensor_tensor(carrier[:, 0:1], carrier[:, 1:2], carrier[:, 2:3], ALU.add).then_inc(m_own, 1)
                    for i in range(B5):
                        gp.indirect_dma_start(rec_dram[:, :], bass.IndirectOffsetOnAxis(ap=idx5[:, 0, i:i + 1], axis=0),
                                              rec5[:, 0, i, :], None, bounds_check=CAP * NG - 1, oob_is_err=False).then_inc(m_scat, 16)
                    gp.wait_ge(m_scat, b * (16 * B5) + 16 * B5)
                    gp.wait_ge(m_own, batch + 1)
                gp.wait_ge(m_recl, k * 16)
                gp.sem_inc(m_carry, 1)
                gp.inc_swdge_sem([m_scat], [16 * ET], mode="sub")
            gp.wait_ge(s_slot, 1)
            gp.wait_ge(s_xz, 64)
            for j in range(NT):
                n = P if j < NT - 1 else LAST
                gp.indirect_dma_start(xbuf_dram[:, :], bass.IndirectOffsetOnAxis(ap=sidx[0:n, j:j + 1], axis=0),
                                      XN[0:n, j, :], None, bounds_check=NE * XS - 1, oob_is_err=False).then_inc(s_disp, 16)
            for s in range(2):
                gp.wait_ge(s_yst[s], 16 * NE // 2)
            for j in range(NT):
                n = P if j < NT - 1 else LAST
                gp.indirect_dma_start(G[0:n, j, :], None, ybuf_dram[:, :],
                                      bass.IndirectOffsetOnAxis(ap=gidx[0:n, j:j + 1], axis=0)).then_inc(s_gat[j], 16)

        @block.scalar
        def _(act):
            act.wait_ge(s_prep, 1)

            def batch(b, q):
                if b >= 2:
                    act.wait_ge(s_scat[q], 16 * B5 * (b // 2))
                nc.scalar.copy(rec5[:, q, :, :], rec[:, ds(b * B5, B5), :]).then_inc(s_rec, 1)
            for b in range(3):
                batch(b, b % 2)

            act.wait_ge(s_wt, NTR)
            for to, bank in ((wkvT[:, 0, :], ps[:, 4, :]), (wkvT[:, 1, :], ps[:, 5, :]),
                             (woT, ps[:, 6, :].rearrange("p (r n) -> p r n", r=2)), (W0T[:, :, :], ps[:, 7, 0:2 * P].rearrange("p (r n) -> p r n", r=2)),
                             (W1T[:, :], ps[:, 7, 2 * P:3 * P]), (b1T[:, :, :], ps[:, 7, 3 * P:3 * P + 64].rearrange("p (f e) -> p f e", e=NE))):
                nc.scalar.copy(to, bank).then_inc(s_wtc, 1)

            def record(m, k, q):
                act.wait_ge(s_scat[q], (m + (1 if q == 0 else 0)) * (16 * B5))
                nc.scalar.copy(rec5[:, q, :, :], rec[:, ds((m * 2 + k) * B5, B5), :]).then_inc(s_rec, 1)
            with act.Fori(1, STATS_M) as m:
                record(m, 1, 1)
                record(m, 2, 0)
            act.wait_ge(s_var, 1)
            nc.scalar.activation(lnr[:, :], lnb[:, :], ACT.Sqrt).then_inc(s_root, 1)
            with act.Fori(STATS_M, MIX_M) as m:
                record(m, 1, 1)
                record(m, 2, 0)
            act.wait_ge(s_constv, 1)
            act.wait_ge(s_recz, 16)
            act.wait_ge(s_xz, 64)

            def kv(j, first):
                nc.scalar.copy(stage[:, 0, :], XN[:, ds(j, 1), :].rearrange("p a d -> p (a d)")).then_inc(phase["mixa", "staged"], 1)
                act.wait_ge(phase["mixa", "turned"], j + 1)
                nc.scalar.copy(work[:, 0, :], ps[:, 4, 0:D]).then_inc(phase["mixa", "xt"], 1)
                record(j + MIX_M, 1, 1)
                record(j + MIX_M, 2, 0)
                act.wait_ge(phase["mixa", "prod"], j + 1)
                nc.scalar.copy(KC[:, ds(j, 1), :].rearrange("p a d -> p (a d)"), ps[:, 5, :])
                if not first:
                    act.wait_ge(s_sq, j)
                    act.sem_inc(m_carry, 1)
                for h in range(NH):
                    head = nc.scalar.activation(sq[:, 0, h * HD:(h + 1) * HD], ps[:, 5, h * HD:(h + 1) * HD], ACT.Square,
                                                accum_out=hvar[:, ds(j * NH + h, 1)])
                head.then_inc(s_sq, 1)
            act.wait_ge(s_xn, NT)
            kv(0, True)
            with act.Fori(1, NT) as j:
                kv(j, False)
            act.wait_ge(s_hvar, 1)
            nc.scalar.activation(hrs[:, :], hvar[:, :], ACT.Sqrt).then_inc(s_hroot, 1)

            def weigh(j, k, c):
                g0, g1 = PARTS[c][0:2]
                act.wait_ge(s_hot, (j * len(PARTS) + c) * 2 + 1)
                act.sem_inc(m_carry, 1)
                for g in range(g0 + DW, g1):
                    nc.scalar.activation(bc[k][:, g, :], bc[k][:, g, :], ACT.Copy, scale=recL[:, ds(j * NR + g, 1), 2]).then_inc(s_wgt, 1)

            def evac(j, slot, c, first):
                if c == 0 and not first:
                    act.wait_ge(s_ast[slot], (j - slot) * 8)
                for q in range(*PARTS[c][2:4]):
                    w = min(4, NR - 4 * q)
                    act.wait_ge(s_bmm, j * NR + 4 * q + w)
                    dst = ADJ[:, slot, :].rearrange("p (r g) -> p r g", g=NR)[:, :, 4 * q:4 * q + w]
                    nc.scalar.copy(dst, ps[:, q, 0:w * P].rearrange("p (g r) -> p r g", r=P)).then_inc(s_bev, 1)

            def both(j, slot, first):
                for c in range(len(PARTS)):
                    if not (isinstance(j, int) and j == NT - 1):
                        weigh(j + 1, 1 - slot, c)
                    evac(j, slot, c, first)
                    if c == 1:
                        act.wait_ge(phase["mixb", "turned"], j + 1)
                        nc.scalar.copy(work[:, 0, :], ps[:, 7, 0:D]).then_inc(phase["mixb", "xt"], 1)
            for c in range(len(PARTS)):
                weigh(0, 0, c)
            both(0, 0, True)
            both(1, 1, True)
            with act.Fori(1, NT // 2) as i:
                both(i * 2, 0, False)
                both(i * 2 + 1, 1, False)
            both(NT - 1, 0, False)

            act.wait_ge(s_xn, NT)
            for half in range(2):
                def st(j, slot, first):
                    if not (first and half == 0):
                        act.wait_ge(s_tile, half * NT + j - SLOTS + 1)
                    nc.scalar.copy(stage[:, slot, :], XN[:, ds(j, 1), :].rearrange("p a d -> p (a d)")).then_inc(s_stage, 1)
                for j in range(SLOTS):
                    st(j, j, True)
                with act.Fori(1, NT // SLOTS) as i:
                    for j in range(SLOTS):
                        st(i * SLOTS + j, j, False)
                act.wait_ge(s_tile, (half + 1) * NT)
                for dd in range(2):
                    for q in range(4):
                        c = (half * 4 + q) * CHUNK
                        nc.scalar.copy(HT[:, dd, c:c + CHUNK], ps[:, dd * 4 + q, 0:CHUNK]).then_inc(s_acc, 1)

            def tanh(l):
                def step(j, s):
                    act.wait_ge(s_sum[l], j + 1)
                    t = P01[:, ds(j, 1), l * H:(l + 1) * H].rearrange("p a d -> p (a d)")
                    nc.scalar.activation(t, t, ACT.Tanh).then_inc(s_tanh[l], 1)
                return step

            def tanh0(j, s):
                act.wait_ge(s_sum[0], j + 1)
                nc.scalar.activation(work[:, s, 0:H], work[:, s, 0:H], ACT.Tanh).then_inc(s_tanh[0], 1)

            for l in (0, 1):
                def st(j, s):
                    if l == 0:
                        if isinstance(j, int):
                            act.wait_ge(phase["hn", "turned"], NT)
                            act.wait_ge(phase["hn", "read"], NT)
                        else:
                            act.wait_ge(s_zt[0], j - SLOTS + 1)
                        nc.scalar.copy(stage[:, s, 0:H], Y[:, ds(j, 1), :].rearrange("p a d -> p (a d)")).then_inc(s_stage, 1)
                    else:
                        if isinstance(j, int):
                            act.wait_ge(phase["sm0", "turned"], NT)
                            act.wait_ge(s_sm[0], NT)
                        else:
                            act.wait_ge(s_zt[1], j - SLOTS + 1)
                        nc.scalar.copy(stage[:, s, 0:H], P01[:, ds(j, 1), 0:H].rearrange("p a d -> p (a d)")).then_inc(s_stage, 1)
                for j in range(SLOTS):
                    st(j, j)
                if l == 1:
                    tiles(act, tanh0)
                with act.Fori(1, NT // SLOTS) as i:
                    for j in range(SLOTS):
                        st(i * SLOTS + j, j)
                act.wait_ge(s_zt[l], NT)
                for q in range(8):
                    c = q * CHUNK
                    if l == 0:
                        nc.scalar.activation(HT[:, 0, c:c + CHUNK], ps[:, q, 0:CHUNK], ACT.Identity, bias=cols[:, 0:1]).then_inc(s_z[l], 1)
                    else:
                        nc.scalar.copy(HT[:, 0, c:c + CHUNK], ps[:, q, 0:CHUNK]).then_inc(s_z[l], 1)

                def ex(j, s):
                    act.wait_ge(s_nm[l], j + 1)
                    ge(act, s_sm[0] if l == 0 else s_sum[1], j - SLOTS + 1)
                    nc.scalar.activation(work[:, s, 0:H], ps[:, s % 3, 0:H], ACT.Exp, bias=nmx[:, s:s + 1],
                                         accum_out=rsum[:, s:s + 1]).then_inc(s_ex[l], 1)
                if l == 0:
                    tiles(act, ex)
                else:
                    tiles_ahead(act, ex, tanh(1))
            act.wait_ge(s_var, 2)
            nc.scalar.activation(lnr[:, :], lnb[:, :], ACT.Sqrt).then_inc(s_root, 1)
            def logits(c):
                w = min(NP - c * 512, 512)
                act.wait_ge(phase["gate", "prod"], c + 1)
                nc.scalar.copy(LT[:, c * 512:c * 512 + w], ps[0:NE, c % 2, 0:w]).then_inc(phase["gate", "read"], 1)
            for j in range(NT):
                act.wait_ge(phase["gate", "turned"], j + 1)
                nc.scalar.copy(HT[:, :, j * P:(j + 1) * P], ps[:, 2 + j % SLOTS, 0:D].rearrange("p (c n) -> p c n", c=2)).then_inc(phase["gate", "xt"], 1)
                if j % 4 == 3 and j > 4:
                    logits(j // 4 - 1)
            logits(5)
            logits(6)
            act.wait_ge(s_exp8, 1)
            nc.scalar.activation(ta8, tb8, ACT.Exp).then_inc(s_exp8, 1)

            def rows_out(e, s):
                for c in range(2):
                    act.wait_ge(s_xbt, 2 * e + c + 1)
                    nc.scalar.copy(xbT[:, s, c, :], ps[:, c, :]).then_inc(s_xbv, 1)

            def hidden(e):
                for f in range(8):
                    act.wait_ge(s_hid, 8 * e + f + 1)
                    if f == 0:
                        ge(act, s_y, 4 * e)
                    nc.scalar.activation(hmT[:, f, 0:CAPX], ps[:, 2 + f % 3, 0:CAPX], ACT.Relu, bias=b1T[:, f, ds(e, 1)]).then_inc(s_hidv, 1)
            rows_out(0, 0)
            hidden(0)
            rows_out(1, 1)
            with act.Fori(1, NE // 2) as i:
                hidden(i * 2 - 1)
                rows_out(i * 2, 0)
                hidden(i * 2)
                rows_out(i * 2 + 1, 1)
            hidden(NE - 1)

        @block.vector
        def _(dve):
            v = nc.vector
            chain = [0]

            def link(ins):
                chain[0] += 1
                ins.then_inc(s_dve, 1)
                dve.wait_ge(s_dve, chain[0])

            def norm_scale(n):
                me, se, mo, so = bst[:, :, 1], bst[:, :, 2], bst[:, :, 4], bst[:, :, 5]
                link(v.tensor_tensor(lnm[:, :], me, mo, ALU.add))
                link(v.tensor_scalar(lnm[:, :], lnm[:, :], 0.5, None, ALU.mult))
                link(v.tensor_tensor(lna[:, :], me, mo, ALU.subtract))
                link(v.scalar_tensor_tensor(out=lna[:, :], in0=lna[:, :], scalar=0.25, in1=lna[:, :], op0=ALU.mult, op1=ALU.mult))
                link(v.tensor_tensor(lnb[:, :], se, so, ALU.add))
                link(v.scalar_tensor_tensor(out=lnb[:, :], in0=lnb[:, :], scalar=1.0 / D, in1=lna[:, :], op0=ALU.mult, op1=ALU.add))
                v.tensor_scalar(lnb[:, :], lnb[:, :], EPS, None, ALU.add).then_inc(s_var, 1)
                dve.wait_ge(s_root, n + 1)
                link(v.reciprocal(lna[:, :], lnr[:, :]))
                link(v.tensor_tensor(lna[:, :], lna[:, :], lnb[:, :], ALU.mult))
                link(v.tensor_tensor(lnr[:, :], lnr[:, :], lna[:, :], ALU.add))
                link(v.tensor_scalar(lnr[:, :], lnr[:, :], 0.5, None, ALU.mult))
                link(v.reciprocal(lnr[:, :], lnr[:, :]))

            dve.wait_ge(s_edge, 48)
            v.tensor_copy(srcf, src_i).then_inc(s_dve, 1)
            chain[0] += 1
            link(v.tensor_copy(dstf, dst_i))
            link(v.tensor_scalar(quo, dstf, 1.0 / P, 0.5 / P - 0.5, ALU.mult, ALU.add))
            link(v.tensor_scalar(quo, quo, MAGIC, MAGIC, ALU.add, ALU.subtract))
            link(v.scalar_tensor_tensor(out=rec[:, :, 0], in0=quo, scalar=-float(P), in1=dstf, op0=ALU.mult, op1=ALU.add))
            link(v.tensor_scalar(key[:, 0:ET], quo, float(NR), None, ALU.mult))
            link(v.tensor_scalar(quo, srcf, 1.0 / NR, 0.5 / NR - 0.5, ALU.mult, ALU.add))
            link(v.tensor_scalar(rec[:, :, 1], quo, MAGIC, MAGIC, ALU.add, ALU.subtract))
            link(v.scalar_tensor_tensor(out=quo, in0=rec[:, :, 1], scalar=-float(NR), in1=srcf, op0=ALU.mult, op1=ALU.add))
            link(v.tensor_tensor(key[:, 0:ET], key[:, 0:ET], quo, ALU.add))
            link(v.memset(key[:, ET:ET + AHEAD], -1.0))
            link(v.tensor_copy(rec[:, :, 2], val))
            v.memset(rec[:, :, 3], 0.0).then_inc(s_prep, 1)
            dve.wait_ge(s_const, 6)
            link(v.tensor_copy(iota_g[:, :], iota_i))
            link(v.tensor_copy(iota_n[:, :], iota_i[:, 0:P]))
            link(v.tensor_copy(before[:, :], before_f[:, :]))
            link(v.tensor_scalar(notbefore[:, :], before_f[:, :], -1.0, 1.0, ALU.mult, ALU.add))
            v.tensor_copy(ones_b[:, :], ones_f[:, :]).then_inc(s_constv, 1)
            dve.wait_ge(s_zero, 3)

            def onehot(t, slot):
                v.tensor_scalar(oh[:, slot, 0:NG], iota_g[0:EP, 0:NG], key[:, ds(t, 1)], None, ALU.is_equal).then_inc(s_oh, 1)

            def rank(t, i, par, q):
                dve.wait_ge(s_rank, t + 1)
                v.tensor_tensor_reduce(out=junk[:, par, 0:NG], in0=ps[0:EP, 2 * par:2 * par + 2, :].rearrange("p b n -> p (b n)")[:, 0:NG],
                                       in1=oh[:, i % 5, 0:NG], scale=1.0, scalar=0.0, op0=ALU.mult, op1=ALU.add,
                                       accum_out=pos5[:, q, i % 5:i % 5 + 1]).then_inc(s_rankrd, 1)
                onehot(t + AHEAD, (i + AHEAD) % 5)

            def slots(b, q, wait):
                if wait is not None:
                    dve.wait_ge(s_scat[q], wait)
                dve.wait_ge(s_rankrd, (b + 1) * B5)
                v.scalar_tensor_tensor(out=idx5[:, q, :], in0=pos5[:, q, :], scalar=float(NG),
                                       in1=key[:, ds(b * B5, B5)], op0=ALU.mult, op1=ALU.add).then_inc(s_idx, 1)
                v.tensor_copy(pos_all[:, ds(b * B5, B5)], pos5[:, q, :])

            for i in range(AHEAD):
                onehot(i, i)
            for i in range(B5):
                rank(i, i, i % 2, 0)
            slots(0, 0, None)
            for i in range(B5):
                rank(B5 + i, i, (i + 1) % 2, 1)
            slots(1, 1, None)
            for i in range(B5):
                rank(2 * B5 + i, i, i % 2, 0)
            slots(2, 0, 16 * B5)

            def body(m, between):
                for i in range(B5):
                    rank(m * 10 + 5 + i, i, (1 + i) % 2, 1)
                    if i % 2 == 1:
                        between(i // 2)
                slots(m * 2 + 1, 1, m * (16 * B5))
                for i in range(B5):
                    rank(m * 10 + 10 + i, i, i % 2, 0)
                    if i == 2:
                        between(2)
                slots(m * 2 + 2, 0, (m + 1) * (16 * B5))

            def tile(t, j):
                return t[:, ds(j, 1), :].rearrange("p a d -> p (a d)")

            def take_stats(j):
                v.bn_stats(tile(bst, j), tile(X1, j)).then_inc(s_stats, 1)

            def norm(j):
                v.tensor_scalar(tile(XN, j), tile(X1, j), lnm[:, ds(j, 1)], lnr[:, ds(j, 1)], ALU.subtract, ALU.mult).then_inc(s_xn, 1)

            dve.wait_ge(s_x, 32)
            with dve.Fori(1, STATS_M) as m:
                body(m, lambda n: take_stats(m * 3 - 3 + n))
            take_stats(NT - 1)
            dve.wait_ge(s_wtc, 6)
            for c in range(2):
                link(v.tensor_reduce(hm[:, c, :], wkvT[:, c, :].rearrange("p (h d) -> p h d", d=HD), AX_X, ALU.add))
                link(v.tensor_scalar(hm[:, c, :], hm[:, c, :], 1.0 / HD, None, ALU.mult))
                w = wkvT[:, c, :].rearrange("p (h d) -> p h d", d=HD)
                link(v.tensor_tensor(w, w, hm[:, c, :].unsqueeze(2).to_broadcast([P, NH, HD]), ALU.subtract))
            v.memset(zpad[:, :], 0.0).then_inc(s_wtv, 1)
            dve.wait_ge(s_stats, NT)
            norm_scale(0)
            with dve.Fori(STATS_M, MIX_M) as m:
                body(m, lambda n: norm((m - STATS_M) * 3 + n))
            for j in range((MIX_M - STATS_M) * 3, NT):
                norm(j)

            with dve.Fori(MIX_M, NB // 2) as m:
                body(m, lambda n: None)

            dve.wait_ge(s_rankrd, ET)
            link(v.engine_nop())
            v.tensor_reduce(pmax[:, :], pos_all, AX_X, ALU.max).then_inc(s_max, 1)
            dve.wait_ge(s_max, 2)
            link(v.tensor_reduce(prow[:, 0:1], ps[0:1, 7, 0:EP], AX_X, ALU.max))
            link(v.tensor_scalar(prow[:, 0:1], prow[:, 0:1], 1.0 / CAP, 0.5 / CAP + 0.5, ALU.mult, ALU.add))
            link(v.tensor_scalar(prow[:, 0:1], prow[:, 0:1], MAGIC, MAGIC, ALU.add, ALU.subtract))
            v.tensor_copy(rounds[:, :], prow[:, 0:1]).then_inc(s_rounds, 1)

            dve.wait_ge(s_sq, NT)
            link(v.tensor_scalar(hvar[:, :], hvar[:, :], 1.0 / HD, EPS, ALU.mult, ALU.add))
            v.engine_nop().then_inc(s_hvar, 1)
            dve.wait_ge(s_hroot, 1)
            link(v.reciprocal(hta, hrs[:, :]))
            link(v.tensor_tensor(hta, hta, hvar[:, :], ALU.mult))
            link(v.tensor_tensor(hrs[:, :], hrs[:, :], hta, ALU.add))
            link(v.tensor_scalar(hrs[:, :], hrs[:, :], 0.5, None, ALU.mult))
            link(v.reciprocal(hrs[:, :], hrs[:, :]))

            def normed(j, s):
                ge(dve, s_kvt, j - SLOTS + 1)
                v.tensor_tensor(khat[:, s, :].rearrange("p (h d) -> p h d", d=HD),
                                KC[:, ds(j, 1), :].rearrange("p a (h d) -> p (a h) d", d=HD),
                                hrs[:, ds(j * NH, NH)].unsqueeze(2).to_broadcast([P, NH, HD]), ALU.mult).then_inc(s_khat, 1)
            tiles(dve, normed)
            dve.wait_ge(s_gv, 1)
            link(v.tensor_copy(gvb[:, :, :], ps[:, 7, 2 * P:2 * P + 2 * HD].rearrange("p (a e) -> p a e", e=HD)))
            dve.wait_ge(s_kvt, NT)
            for c in range(2):
                sv = ps[:, 6, c * P:(c + 1) * P].rearrange("p (h d) -> p h d", d=HD)
                g_v = gvb[:, 0, :].unsqueeze(1).to_broadcast([P, 2, HD])
                b_v = gvb[:, 1, :].unsqueeze(1).to_broadcast([P, 2, HD])
                t = work[:, 0, 0:P].rearrange("p (h d) -> p h d", d=HD)
                u = work[:, 1, 0:P].rearrange("p (h d) -> p h d", d=HD)
                k2 = kvp[:, c, :].rearrange("p (h d) -> p h d", d=HD)
                link(v.tensor_tensor(k2, ps[:, 4 + c, 0:P].rearrange("p (h d) -> p h d", d=HD), g_v, ALU.mult))
                link(v.tensor_copy(kvc[:, c, 0:1], ps[:, 2 + c, 0:1]))
                link(v.tensor_scalar(t, b_v, kvc[:, c, 0:1], None, ALU.mult))
                link(v.tensor_tensor(k2, k2, t, ALU.add))
                link(v.tensor_scalar(k2, k2, cols[:, 1:2], None, ALU.mult))
                link(v.tensor_tensor(t, sv, g_v, ALU.mult))
                link(v.tensor_scalar(u, b_v, float(N), None, ALU.mult))
                link(v.tensor_tensor(t, t, u, ALU.add))
                link(v.tensor_scalar(t, t, cols[:, 2:3], None, ALU.mult))
                link(v.tensor_tensor(k2, k2, t, ALU.add))
                link(v.tensor_scalar(k2, k2, 1.0 / N, None, ALU.mult))
                link(v.memset(kvp[0:HD, c, HD:P], 0.0))
                link(v.memset(kvp[HD:P, c, 0:HD], 0.0))
            v.engine_nop().then_inc(s_kvp, 1)
            dve.wait_ge(s_t1, 1)
            v.tensor_copy(work[:, 0, :], ps[:, 0, 0:D])
            v.tensor_copy(work[:, 1, :], ps[:, 1, 0:D]).then_inc(s_t1v, 1)
            dve.wait_ge(s_m, 1)
            v.tensor_copy(M[:, 0, :], ps[:, 2, 0:D])
            v.tensor_copy(M[:, 1, :], ps[:, 3, 0:D]).then_inc(s_mv, 1)

            def mixed(j):
                dve.wait_ge(phase["mixb", "prod"], j + 1)
                v.tensor_tensor(tile(X1, j), tile(X1, j), ps[:, 7, D:2 * D], ALU.add).then_inc(phase["mixb", "read"], 1)

            dve.wait_ge(s_recl, 16)

            def pairs(j, k, first):
                for g0, g1, _, _ in PARTS:
                    if not first:
                        dve.wait_ge(s_bmm, (j - 2) * NR + g1)
                        if g0 == PARTS[1][0]:
                            mixed(j - 2)
                    gw = g0 + DW
                    for g in range(g0, gw):
                        n = ds(j * NR + g, 1)
                        v.tensor_scalar(bc[k][:, g, :], iota_n[:, :], recL[:, n, 0], recL[:, n, 2], ALU.is_equal, ALU.mult)
                    for to, field, a0 in ((bc, 0, gw), (br, 1, g0)):
                        v.tensor_tensor(to[k][:, a0:g1, :], iota_n[:, :].unsqueeze(1).to_broadcast([P, g1 - a0, P]),
                                        recL[:, ds(j * NR + a0, g1 - a0), field].unsqueeze(2).to_broadcast([P, g1 - a0, P]),
                                        ALU.is_equal).then_inc(s_hot, 1)
            pairs(0, 0, True)
            pairs(1, 1, True)
            with dve.Fori(1, NT // 2) as i:
                pairs(i * 2, 0, False)
                pairs(i * 2 + 1, 1, False)
            pairs(NT - 1, 0, False)
            mixed(NT - 2)
            mixed(NT - 1)
            dve.wait_ge(s_bmm, NG)
            v.memset(HT[:, :, 8 * CHUNK:NP], 0.0).then_inc(s_tail, 1)

            dve.wait_ge(s_rounds, 1)
            with more_rounds(dve) as k:
                v.tensor_scalar(pos_all, pos_all, -float(CAP), None, ALU.add).then_inc(m_dve, 1)
                dve.wait_ge(m_dve, k * 3 - 2)
                v.tensor_scalar(big_all, pos_all, 0.0, 1.0e8, ALU.is_lt, ALU.mult).then_inc(m_dve, 1)
                v.scalar_tensor_tensor(out=low_all, in0=pos_all, scalar=float(NG), in1=key[:, 0:ET], op0=ALU.mult, op1=ALU.add).then_inc(m_dve, 1)
                dve.wait_ge(m_dve, k * 3)
                v.tensor_tensor(idx_all, low_all, big_all, ALU.add).then_inc(m_idx, 1)
                dve.wait_ge(m_recl, k * 16)
                dve.sem_inc(m_carry, 1)
                with dve.Fori(0, NT) as j:
                    tile = k * NT + j - NT
                    dve.wait_ge(m_load, tile * 16 + 16)
                    dve.sem_inc(m_carry, 1)
                    with dve.Fori(0, NR) as r:
                        block_n = tile * NR + r
                        g = ds(j * NR + r, 1)
                        v.tensor_scalar(ohc[:, 0, :], iota_n[:, :], recL[:, g, 0], recL[:, g, 2], ALU.is_equal, ALU.mult)
                        v.tensor_scalar(ohr[:, 0, :], iota_n[:, :], recL[:, g, 1], None, ALU.is_equal).then_inc(m_pair, 1)
                        dve.wait_ge(m_mm, block_n + 1)
                        part = ADJ[:, 0, :].rearrange("p (r g) -> p r g", g=NR)[:, :, ds(r, 1)].rearrange("p r a -> p (r a)")
                        v.tensor_tensor(part, part, ps[:, 7, 0:P], ALU.add).then_inc(m_add, 1)
                        dve.wait_ge(m_add, block_n + 1)

            def hrow(j, s):
                dve.wait_ge(phase["hn", "turned"], j + 1)
                v.tensor_copy(XN[:, j, :], ps[:, s, 0:D])
                v.tensor_copy(Y[:, j, :], ps[:, s, D:D + H]).then_inc(phase["hn", "read"], 1)
            for j in range(NT):
                hrow(j, j % 7)

            for l in (0, 1):
                def mx(j, s):
                    dve.wait_ge(phase[f"sm{l}", "turned"], j + 1)
                    ge(dve, s_ex[l], j - SLOTS + 1)
                    v.tensor_reduce(nmx[:, s:s + 1], ps[:, s % 3, 0:H], AX_X, ALU.max, negate=True).then_inc(s_nm[l], 1)

                def scaled(j, s):
                    dve.wait_ge(s_ex[l], j + 1)
                    v.reciprocal(rrec[:, s:s + 1], rsum[:, s:s + 1]).then_inc(s_rr[l], 1)
                    dve.wait_ge(s_rr[l], j + 1)
                    o = P01[:, ds(j, 1), l * H:(l + 1) * H].rearrange("p a d -> p (a d)")
                    if l == 0:
                        v.tensor_scalar(o, work[:, s, 0:H], rrec[:, s:s + 1], None, ALU.mult).then_inc(s_sm[0], 1)
                    else:
                        v.scalar_tensor_tensor(out=o, in0=work[:, s, 0:H], scalar=rrec[:, s:s + 1],
                                               in1=XN[:, ds(j, 1), H:2 * H].rearrange("p a d -> p (a d)"),
                                               op0=ALU.mult, op1=ALU.add).then_inc(s_sum[1], 1)
                tiles_ahead(dve, mx, scaled)
                if l == 0:
                    def summed(j, s):
                        if isinstance(j, int) and j < SLOTS:
                            dve.wait_ge(s_sm[0], NT)
                        else:
                            dve.wait_ge(s_x1h, j - SLOTS + 1)
                        v.tensor_tensor(work[:, s, 0:H], P01[:, ds(j, 1), 0:H].rearrange("p a d -> p (a d)"),
                                        XN[:, ds(j, 1), 0:H].rearrange("p a d -> p (a d)"), ALU.add).then_inc(s_sum[0], 1)

                    def added0(j, s):
                        dve.wait_ge(s_tanh[0], j + 1)
                        xj = X1[:, ds(j, 1), 0:H].rearrange("p a d -> p (a d)")
                        v.tensor_tensor(xj, xj, work[:, s, 0:H], ALU.add).then_inc(s_x1h, 1)
                    tiles_ahead(dve, summed, added0)

            def added(j, s):
                dve.wait_ge(s_tanh[1], j + 1)
                xj = X1[:, ds(j, 1), H:2 * H].rearrange("p a d -> p (a d)")
                v.tensor_tensor(xj, xj, P01[:, ds(j, 1), H:2 * H].rearrange("p a d -> p (a d)"), ALU.add).then_inc(s_x1, 1)

            def stats(j, s):
                dve.wait_ge(s_x1, j + 1)
                v.bn_stats(bst[:, ds(j, 1), :].rearrange("p a d -> p (a d)"), X1[:, ds(j, 1), :].rearrange("p a d -> p (a d)")).then_inc(s_stats, 1)
            dve.wait_ge(s_x1h, NT)
            tiles_ahead(dve, added, stats)
            dve.wait_ge(s_stats, 2 * NT)
            norm_scale(1)
            with dve.Fori(0, NT) as j:
                v.tensor_scalar(XN[:, ds(j, 1), :].rearrange("p a d -> p (a d)"), X1[:, ds(j, 1), :].rearrange("p a d -> p (a d)"),
                                lnm[:, ds(j, 1)], lnr[:, ds(j, 1)], ALU.subtract, ALU.mult).then_inc(s_xn2, 1)

            dve.wait_ge(phase["gate", "back"], NT)
            link(v.tensor_copy(LG[:, :, :], ps[:, 7, 0:NT * NE].rearrange("p (t e) -> p t e", e=NE)))
            best, total, eid, pos, keep = (rt[:, i, :] for i in range(5))

            def wide(t):
                return t.unsqueeze(2).to_broadcast([P, NT, NE])
            iota8 = iota_n[:, 0:NE].unsqueeze(1).to_broadcast([P, NT, NE])
            link(v.tensor_reduce(best, LG[:, :, :], AX_X, ALU.max))
            link(v.tensor_tensor(tb8, LG[:, :, :], wide(best), ALU.subtract))
            v.engine_nop().then_inc(s_exp8, 1)
            link(v.tensor_scalar(tc8, tb8, 0.0, float(NE), ALU.is_lt, ALU.mult))
            link(v.tensor_tensor(tc8, tc8, iota8, ALU.add))
            link(v.tensor_reduce(eid, tc8, AX_X, ALU.min))
            link(v.tensor_tensor(OH8[:, :, :], iota8, wide(eid), ALU.is_equal))
            v.engine_nop().then_inc(s_one8, 1)
            dve.wait_ge(s_exp8, 2)
            link(v.tensor_reduce(total, ta8, AX_X, ALU.add))
            link(v.reciprocal(total, total))
            dve.wait_ge(s_cnt, 1)
            link(v.tensor_copy(tb8, ps[:, 1, 0:NT * NE].rearrange("p (t e) -> p t e", e=NE)))
            for e in range(NE):
                v.tensor_tensor_scan(out=tc8[:, :, e], data0=ones_f[:, 0:NT], data1=tb8[:, :, e], initial=0.0, op0=ALU.mult, op1=ALU.add)
            link(v.engine_nop())
            link(v.tensor_tensor(tc8, tc8, tb8, ALU.subtract))
            link(v.tensor_tensor(tc8, tc8, ps[:, 0, 0:NT * NE].rearrange("p (t e) -> p t e", e=NE), ALU.add))
            link(v.tensor_tensor(tc8, tc8, OH8[:, :, :], ALU.mult))
            link(v.tensor_reduce(pos, tc8, AX_X, ALU.add))
            link(v.tensor_scalar(keep, pos, float(CAPX), None, ALU.is_le))
            link(v.tensor_tensor(kp[:, :], keep, total, ALU.mult))
            link(v.tensor_scalar(total, pos, float(CAPX), -1.0, ALU.min, ALU.add))
            link(v.scalar_tensor_tensor(out=gidx[:, :], in0=eid, scalar=float(XS), in1=total, op0=ALU.mult, op1=ALU.add))
            link(v.tensor_scalar(keep, keep, -1.0e6, 1.0e6 - 1.0, ALU.mult, ALU.add))
            link(v.tensor_tensor(pos, pos, keep, ALU.add))
            link(v.scalar_tensor_tensor(out=sidx[:, :], in0=eid, scalar=float(XS), in1=pos, op0=ALU.mult, op1=ALU.add))
            link(v.memset(big[:, :], 10000.0))
            link(v.memset(nbig[:, :], -10000.0))
            v.engine_nop().then_inc(s_slot, 1)

            def yblock(e, s):
                for c in range(4):
                    n = min(P, CAPX - c * P)
                    dve.wait_ge(s_y, 4 * e + c + 1)
                    if c == 0:
                        ge(dve, s_yst[s], 16 * ((e - s) // 2) if isinstance(e, int) else yblock.turns)
                    v.tensor_tensor(ybs[0:n, s, c, :], ps[0:n, 5 + c % 2, 0:D], b2_b[0:n, ds(e * D, D)], ALU.add).then_inc(s_yv, 1)
            link(v.memset(ybs, 0.0))
            link(v.memset(sums[:, :], 0.0))
            dve.wait_ge(s_b2, 16)
            yblock(0, 0)
            yblock(1, 1)
            with dve.Fori(1, NE // 2) as i:
                yblock.turns = i * 16
                yblock(i * 2, 0)
                yblock(i * 2 + 1, 1)
            for j in range(NT):
                n = P if j < NT - 1 else LAST
                dve.wait_ge(s_gat[j], 16)
                v.scalar_tensor_tensor(out=XN[0:n, j, :], in0=G[0:n, j, :], scalar=kp[0:n, j:j + 1], in1=X1[0:n, j, :],
                                       op0=ALU.mult, op1=ALU.add, accum_out=sums[0:n, j:j + 1]).then_inc(s_fin, 1)
            dve.wait_ge(s_fin, NT)
            link(v.tensor_scalar(sums[:, :], sums[:, :], 0.0, None, ALU.mult))
            v.tensor_reduce(check[:, :], sums[:, :], AX_X, ALU.add).then_inc(s_check, 1)
            dve.wait_ge(s_check, 2)
            v.tensor_scalar(odd[:, :], ps[0:1, 0, 0:1], 0.0, None, ALU.not_equal).then_inc(s_odd, 1)
            dve.wait_ge(s_odd, 1)
            with dve.If(dve.value_load(odd[0:1, 0:1], min_val=0, max_val=1) > 0):
                dve.wait_ge(s_out, 16 * NT)
                for j in range(NT):
                    n = P if j < NT - 1 else LAST
                    g = G[0:n, j, :]
                    link(v.tensor_scalar(g, g, kp[0:n, j:j + 1], None, ALU.mult))
                    link(v.tensor_scalar(nanm[0:n, 0, :], g, FMAX, None, ALU.is_gt))
                    link(v.tensor_scalar(nanm[0:n, 1, :], g, -FMAX, None, ALU.is_lt))
                    link(v.copy_predicated(g, nanm[0:n, 0, :], big[0:n, :].to_broadcast([n, D])))
                    link(v.copy_predicated(g, nanm[0:n, 1, :], nbig[0:n, :].to_broadcast([n, D])))
                    link(v.tensor_tensor(nanm[0:n, 0, :], g, g, ALU.not_equal))
                    link(v.copy_predicated(g, nanm[0:n, 0, :], zpad[0:n, :].to_broadcast([n, D])))
                    v.tensor_tensor(XN[0:n, j, :], X1[0:n, j, :], g, ALU.add).then_inc(s_fixed, 1)

        @block.tensor
        def _(pe):
            pe.wait_ge(s_constv, 1)

            def ranks(t, i, par, first):
                acc = ps[0:EP, 2 * par:2 * par + 2, :].rearrange("p b n -> p (b n)")
                start = first and t < 2
                if not start:
                    pe.wait_ge(s_rankrd, t - 1)
                pe.wait_ge(s_oh, t + 1)
                for n, (lhs, s) in enumerate(((notbefore, (i - 2) % 5), (ones_b, (i - 1) % 5), (before, i % 5))):
                    for c0, c1 in ((0, 512), (512, NG)):
                        last = nc.tensor.matmul(acc[:, c0:c1], lhs[0:EP, 0:EP], oh[:, s, c0:c1],
                                                start=bool(start and n == 0), stop=True, skip_group_check=True)
                last.then_inc(s_rank, 1)
            for t in range(3 * B5):
                ranks(t, t % 5, t % 2, True)

            def flip(dst, src, n=P):
                return nc.tensor.transpose(dst, src, ident[0:n, 0:n])
            pe.wait_ge(s_w, 16 * NWL)
            for w, name in enumerate((wk_n, wv_n)):
                for r in range(2):
                    for c in range(2):
                        flip(ps[:, 4 + c, w * D + r * P:w * D + (r + 1) * P], name[:, r, c * P:(c + 1) * P]).then_inc(s_wt, 1)
            for r in range(2):
                for c in range(2):
                    flip(ps[:, 6, c * D + r * P:c * D + (r + 1) * P], wo_n[:, r, c * P:(c + 1) * P]).then_inc(s_wt, 1)
            for c in range(2):
                flip(ps[:, 7, c * P:(c + 1) * P], W0_n[:, c * P:(c + 1) * P]).then_inc(s_wt, 1)
            flip(ps[:, 7, 2 * P:3 * P], W1_n).then_inc(s_wt, 1)
            for f in range(8):
                flip(ps[:, 7, 3 * P + f * NE:3 * P + (f + 1) * NE], b1_n[:, f * P:(f + 1) * P], NE).then_inc(s_wt, 1)

            with pe.Fori(1, MIX_M) as m:
                for i in range(10):
                    ranks(m * 10 + 5 + i, i % 5, (1 + i) % 2, False)
            pe.wait_ge(s_wtv, 1)

            def kv(j, first):
                for i in range(10):
                    ranks((j + MIX_M) * 10 + 5 + i, i % 5, (1 + i) % 2, False)
                    if i == 2:
                        pe.wait_ge(phase["mixa", "staged"], j + 1)
                        flip(ps[:, 4, 0:P], stage[:, 0, 0:P])
                        flip(ps[:, 4, P:2 * P], stage[:, 0, P:2 * P]).then_inc(phase["mixa", "turned"], 1)
                    if i == 5:
                        pe.wait_ge(phase["mixa", "xt"], j + 1)
                        if not first:
                            pe.wait_ge(s_sq, j)
                    if i >= 5 and i < 9:
                        for c in range(2):
                            last = nc.tensor.matmul(ps[:, 5, (i - 5) * P:(i - 4) * P], work[:, 0, c * P:(c + 1) * P],
                                                    wkvT[:, c, (i - 5) * P:(i - 4) * P], start=(c == 0), stop=(c == 1), skip_group_check=True)
                last.then_inc(phase["mixa", "prod"], 1)
            kv(0, True)
            with pe.Fori(1, NT) as j:
                kv(j, False)

            def blocks(j, par, first):
                starts = [part[0] for part in PARTS]
                weighed = 0
                for g in range(NR):
                    q, k = g // 4, g % 4
                    if g in starts:
                        c = starts.index(g)
                        pe.wait_ge(s_hot, (j * len(PARTS) + c) * 2 + 2)
                    if k == 0 and not first:
                        pe.wait_ge(s_bev, (j - 1) * 7 + q + 1)
                    if g >= starts[c] + DW:
                        weighed += 1
                        pe.wait_ge(s_wgt, j * (NR - DW * len(PARTS)) + weighed)
                    nc.tensor.matmul(ps[:, q, k * P:(k + 1) * P], bc[par][:, g, :], br[par][:, g, :], start=True, stop=True).then_inc(s_bmm, 1)
                    if g == 11:
                        pe.wait_ge(phase["mixb", "staged"], j + 1)
                        if not (isinstance(j, int) and j == 0):
                            pe.wait_ge(phase["mixb", "read"], j)
                        flip(ps[:, 7, 0:P], stage[:, 0, 0:P])
                        flip(ps[:, 7, P:2 * P], stage[:, 0, P:2 * P]).then_inc(phase["mixb", "turned"], 1)
                    if g == 20:
                        pe.wait_ge(phase["mixb", "xt"], j + 1)
                        o = ps[:, 7, D:2 * D]
                        nc.tensor.matmul(o, work[:, 0, 0:P], M[:, 0, :], start=True, stop=False, skip_group_check=True)
                        nc.tensor.matmul(o, work[:, 0, P:2 * P], M[:, 1, :], start=False, stop=False, skip_group_check=True)
                        nc.tensor.matmul(o, ones_f[0:1, :], bo_r, start=False, stop=True, skip_group_check=True).then_inc(phase["mixb", "prod"], 1)
            nc.tensor.matmul(ps[:, 7, 2 * P:2 * P + 2 * HD], ones_f[0:1, :], rows[:, 2 * D + NE:2 * D + NE + 2 * HD], start=True, stop=True).then_inc(s_gv, 1)
            pe.wait_ge(s_rankrd, ET)
            pe.wait_ge(s_max, 1)
            nc.tensor.transpose(ps[0:1, 7, 0:EP], pmax[:, :], ident[0:EP, 0:EP]).then_inc(s_max, 1)
            def warm(n):
                for _ in range(n):
                    nc.tensor.matmul(ps[:, 0, :], ones_b[:, :], ones_b[:, :].unsqueeze(1).to_broadcast([P, 4, P]), start=True, stop=True)
            warm(24)

            def kvprod(j, s):
                pe.wait_ge(s_khat, j + 1)
                first = isinstance(j, int) and j == 0
                for c in range(2):
                    kh = khat[:, s, c * P:(c + 1) * P]
                    nc.tensor.matmul(ps[:, 4 + c, 0:P], kh, khat[:, s, D + c * P:D + (c + 1) * P], start=first, stop=True, skip_group_check=True)
                    nc.tensor.matmul(ps[:, 2 + c, 0:1], kh, ones_f[:, 0:1], start=first, stop=True, skip_group_check=True)
                nc.tensor.matmul(ps[:, 6, 0:D], ones_f[:, :], khat[:, s, D:2 * D], start=first, stop=True, skip_group_check=True).then_inc(s_kvt, 1)
            tiles(pe, kvprod)
            warm(32)
            pe.wait_ge(s_kvp, 1)
            for c in range(2):
                last = nc.tensor.matmul(ps[:, c, 0:D], kvp[:, c, :], wq_n[:, c, :], start=True, stop=True)
            last.then_inc(s_t1, 1)
            pe.wait_ge(s_t1v, 1)
            for i in range(2):
                for c in range(2):
                    last = nc.tensor.matmul(ps[:, 2 + i, 0:D], work[:, c, i * P:(i + 1) * P], woT[:, c, :], start=(c == 0), stop=(c == 1))
            last.then_inc(s_m, 1)
            pe.wait_ge(s_mv, 1)
            blocks(0, 0, True)
            blocks(1, 1, False)
            with pe.Fori(1, NT // 2) as i:
                blocks(i * 2, 0, False)
                blocks(i * 2 + 1, 1, False)
            blocks(NT - 1, 0, False)

            pe.wait_ge(s_bev, 7 * NT)
            pe.wait_ge(phase["mixb", "read"], NT)
            with more_rounds(pe) as k:
                with pe.Fori(0, NG) as g:
                    block_n = k * NG + g - NG
                    pe.wait_ge(m_pair, block_n + 1)
                    nc.tensor.matmul(ps[:, 7, 0:P], ohc[:, 0, :], ohr[:, 0, :], start=True, stop=True).then_inc(m_mm, 1)
                    pe.wait_ge(m_add, block_n + 1)

            def spmm1(half):
                def tile(j, slot, loaded, first):
                    pe.wait_ge(s_ald[slot], loaded)
                    pe.wait_ge(s_stage, half * NT + j + 1)
                    for dd in range(2):
                        for q in range(4):
                            last = nc.tensor.matmul(ps[:, dd * 4 + q, 0:CHUNK], stage[:, slot, dd * H:(dd + 1) * H],
                                                    ADJ[:, slot, q * CHUNK:(q + 1) * CHUNK], start=first, stop=True, skip_group_check=True)
                    last.then_inc(s_tile, 1)
                if half == 0:
                    pe.wait_ge(s_bev, 7 * NT)
                else:
                    pe.wait_ge(s_acc, 8)
                r = NT // SLOTS
                for j in range(SLOTS):
                    tile(j, j, (half * r + 1) * 16, j == 0)
                with pe.Fori(1, r) as i:
                    for j in range(SLOTS):
                        tile(i * SLOTS + j, j, (i + half * r + 1) * 16, False)
            spmm1(0)
            spmm1(1)

            pe.wait_ge(s_acc, 16)
            pe.wait_ge(s_tail, 1)
            for j in range(NT):
                b = j % 7
                ge(pe, phase["hn", "read"], j - 6)
                t = [HT[:, c, j * P:(j + 1) * P] for c in range(2)]
                flip(ps[:, b, 0:P], t[0])
                flip(ps[:, b, P:2 * P], t[1])
                nc.tensor.matmul(ps[:, b, D:D + H], t[0], W0T[:, 0, :], start=True, stop=False, skip_group_check=True)
                nc.tensor.matmul(ps[:, b, D:D + H], t[1], W0T[:, 1, :], start=False, stop=True, skip_group_check=True).then_inc(phase["hn", "turned"], 1)
            pe.wait_ge(phase["hn", "read"], NT)

            for l in (0, 1):
                def ztile(j, s):
                    k = (2 + l) * (NT // SLOTS)
                    pe.wait_ge(s_ald[s], (k + 1) * 16 if isinstance(j, int) else (ztile.i + k + 1) * 16)
                    pe.wait_ge(s_stage, (2 + l) * NT + j + 1)
                    first = isinstance(j, int) and j == 0
                    for q in range(8):
                        last = nc.tensor.matmul(ps[:, q, 0:CHUNK], stage[:, s, 0:H], ADJ[:, s, q * CHUNK:(q + 1) * CHUNK],
                                                start=first, stop=True, skip_group_check=True)
                    last.then_inc(s_zt[l], 1)
                for j in range(SLOTS):
                    ztile(j, j)
                with pe.Fori(1, NT // SLOTS) as i:
                    ztile.i = i
                    for s in range(SLOTS):
                        ztile(i * SLOTS + s, s)

                for j in range(NT):
                    pe.wait_ge(s_z[l], min(max(3, (j * P + P - 1) // CHUNK + 1), 8))
                    ge(pe, s_ex[l], j - 1)
                    o = ps[:, j % SLOTS % 3, 0:H]
                    t = HT[:, 0, j * P:(j + 1) * P]
                    if l == 0:
                        flip(o, t).then_inc(phase["sm0", "turned"], 1)
                    else:
                        nc.tensor.matmul(o, t, W1T[:, :], start=True, stop=False)
                        nc.tensor.matmul(o, ones_f[0:1, :], gb1_r, start=False, stop=True).then_inc(phase["sm1", "turned"], 1)
                pe.wait_ge(s_ex[l], NT)

            def logits(c):
                w = min(NP - c * 512, 512)
                pe.wait_ge(phase["gate", "xt"], min(4 * c + 4, NT))
                ge(pe, phase["gate", "read"], c - 1)
                o = ps[0:NE, c % 2, 0:w]
                for k in range(2):
                    nc.tensor.matmul(o, gate_w[:, k, :], HT[:, k, c * 512:c * 512 + w], start=(k == 0), stop=False)
                nc.tensor.matmul(o, gate_b, ones_f[0:1, :].unsqueeze(1).to_broadcast([1, w // P, P]), start=False, stop=True).then_inc(phase["gate", "prod"], 1)
            for j in range(NT):
                pe.wait_ge(s_xn2, j + 1)
                ge(pe, phase["gate", "xt"], j - SLOTS + 1)
                flip(ps[:, 2 + j % SLOTS, 0:P], XN[:, j, 0:P])
                flip(ps[:, 2 + j % SLOTS, P:2 * P], XN[:, j, P:2 * P]).then_inc(phase["gate", "turned"], 1)
                if j % 4 == 1 and j > 4:
                    logits(j // 4 - 1)
            logits(5)
            logits(6)
            for j in range(NT):
                pe.wait_ge(phase["gate", "read"], j // 4 + 1)
                flip(ps[:, 7, j * NE:(j + 1) * NE], LT[:, j * P:(j + 1) * P], NE).then_inc(phase["gate", "back"], 1)
            pe.wait_ge(s_one8, 1)
            oh8 = OH8[:, :, :].rearrange("p t e -> p (t e)")
            nc.tensor.matmul(ps[:, 0, 0:NT * NE], upto[:, :], oh8, start=True, stop=True)
            nc.tensor.matmul(ps[:, 1, 0:NT * NE], ones_f[:, :], oh8, start=True, stop=True).then_inc(s_cnt, 1)

            pe.wait_ge(s_slot, 1)

            def rows_in(e, s, loaded):
                pe.wait_ge(s_wl[s], loaded)
                ge(pe, s_xbv, 2 * e)
                for c in range(2):
                    for b in range(4):
                        last = flip(ps[:, c, b * P:(b + 1) * P], xbs[:, s, b, c * P:(c + 1) * P])
                    last.then_inc(s_xbt, 1)

            def up(e, s):
                pe.wait_ge(s_xbv, 2 * e + 2)
                for f in range(8):
                    ge(pe, s_hidv, 8 * e + f - 2)
                    for c in range(2):
                        last = nc.tensor.matmul(ps[:, 2 + f % 3, 0:CAPX], w1s[:, s, c, f * P:(f + 1) * P], xbT[:, s, c, 0:CAPX],
                                                start=(c == 0), stop=(c == 1))
                    last.then_inc(s_hid, 1)

            def down(e, s):
                pe.wait_ge(s_hidv, 8 * e + 8)
                for c in range(4):
                    n = min(P, CAPX - c * P)
                    ge(pe, s_yv, 4 * e + c - 1)
                    o = ps[0:n, 5 + c % 2, 0:D]
                    for f in range(8):
                        last = nc.tensor.matmul(o, hmT[:, f, c * P:c * P + n], w2s[:, s, f, :], start=(f == 0), stop=(f == 7))
                    last.then_inc(s_y, 1)
            rows_in(0, 0, 48)
            up(0, 0)
            rows_in(1, 1, 48)
            down(0, 0)
            with pe.Fori(1, NE // 2) as i:
                up(i * 2 - 1, 1)
                rows_in(i * 2, 0, (i + 1) * 48)
                down(i * 2 - 1, 1)
                up(i * 2, 0)
                rows_in(i * 2 + 1, 1, (i + 1) * 48)
                down(i * 2, 0)
            up(NE - 1, 1)
            down(NE - 1, 1)
            pe.wait_ge(s_check, 1)
            nc.tensor.matmul(ps[0:1, 0, 0:1], check[:, :], ones_f[:, 0:1], start=True, stop=True).then_inc(s_check, 1)


_INS = ["x", "src", "dst", "edge_weight", "L0_gnn_W0", "L0_gnn_b0", "L0_gnn_W1", "L0_gnn_b1", "L0_mix_wq", "L0_mix_wk", "L0_mix_wv",
        "L0_mix_wo", "L0_mix_bo", "L0_mix_ln_k_g", "L0_mix_ln_k_b", "L0_mix_ln_v_g", "L0_mix_ln_v_b", "L0_ffn_gate_w", "L0_ffn_gate_b",
        "L0_ffn_w1", "L0_ffn_b1", "L0_ffn_w2", "L0_ffn_b2"]


def kernel(**inputs):
    import numpy as np
    import concourse.bacc as bacc
    from concourse.bass_utils import run_bass_kernel_spmd

    nc = bacc.Bacc("TRN2", target_bir_lowering=False, num_devices=1)
    arrays, aps = {}, {}
    for name in _INS:
        v = np.ascontiguousarray(inputs[name])
        arrays[f"in_{name}"] = v
        aps[name] = nc.dram_tensor(f"in_{name}", v.shape, mybir.dt.from_np(v.dtype), kind="ExternalInput").ap()
    out = nc.dram_tensor("out_0", (N, D), F32, kind="ExternalOutput").ap()
    graph_program(nc, aps, out)
    r = run_bass_kernel_spmd(nc, [arrays], core_ids=[0])
    return r.results[0]["out_0"]
```
